# Optimizing a Trainium2 kernel written in Bass

```python
import numpy as np
import jax
import jax.numpy as jnp

def _softmax(x, axis=-1):
    return jax.nn.softmax(x, axis=axis)

def _gelu(x):
    return jax.nn.gelu(x, approximate=True)

def _silu(x):
    return jax.nn.silu(x)

def _sigmoid(x):
    return jax.nn.sigmoid(x)

def _layernorm(x, axis=-1, eps=1e-05):
    m = jnp.mean(x, axis=axis, keepdims=True)
    v = jnp.var(x, axis=axis, keepdims=True)
    return (x - m) / jnp.sqrt(v + eps)

def _scatter_add(tgt, idx, src, axis=0):
    return tgt.at[idx].add(src)

def _segment_sum(src, seg, n):
    return jax.ops.segment_sum(src, seg, n)
kernel_name = 'mk_cond_resid_d2_seqx_r8_453138'

def setup_inputs(seed: int=0):
    np.random.seed(seed)
    _w = jnp.asarray

    def _rec_inputs():
        import jax
        import jax.numpy as jnp
        _rk = jax.random.key(seed)
        x = -0.0005207 + 1.001 * jax.random.normal(jax.random.fold_in(_rk, 1), (64, 32, 512), jnp.float32)
        _lenS = 32 - jax.random.randint(jax.random.fold_in(_rk, 7), (64,), 0, max(1, 32 // 4) + 1, jnp.int32)
        _lenS2 = 32 - jax.random.randint(jax.random.fold_in(_rk, 8), (64,), 0, max(1, 32 // 4) + 1, jnp.int32)
        itok_Bx16_0_63 = jax.random.randint(jax.random.fold_in(_rk, 11), (64, 16), 0, 64, jnp.int32)
        itok_B_207_1644 = jax.random.randint(jax.random.fold_in(_rk, 12), (64,), 207, 1645, jnp.int32)
        itok_B_0_7 = jax.random.randint(jax.random.fold_in(_rk, 13), (64,), 0, 8, jnp.int32)
        itok_B_2182_4065 = jax.random.randint(jax.random.fold_in(_rk, 15), (64,), 2182, 4066, jnp.int32)
        return (x, itok_Bx16_0_63, itok_B_207_1644, itok_B_0_7, itok_B_2182_4065, _lenS)
    x, itok_Bx16_0_63, itok_B_207_1644, itok_B_0_7, itok_B_2182_4065, _lenS = _rec_inputs()

    def _L0_cond_setup():
        import jax, jax.numpy as jnp
        import numpy as np
        B, S, HID = (4, 128, 512)
        D, HQ, HK = (128, 32, 8)
        PAGES, PSIZE, NPP = (64, 32, 16)
        THETA = 10000.0
        EPS = 1e-06
        SCALE = 1.0 / float(np.sqrt(D))

        def _rmsnorm(t, w):
            var = jnp.mean(t * t, axis=-1, keepdims=True)
            return t * jax.lax.rsqrt(var + EPS) * w

        def _rope(t, pos):
            inv_freq = 1.0 / THETA ** (jnp.arange(0, D, 2, dtype=jnp.float32) / D)
            freqs = pos[..., None].astype(jnp.float32) * inv_freq
            cos = jnp.cos(freqs)[:, :, None, :]
            sin = jnp.sin(freqs)[:, :, None, :]
            t1, t2 = (t[..., :D // 2], t[..., D // 2:])
            return jnp.concatenate([t1 * cos - t2 * sin, t2 * cos + t1 * sin], axis=-1)
        key = jax.random.key(seed)
        ks = jax.random.split(key, 10)
        x = jax.random.normal(ks[0], (B, S, HID), jnp.float32)
        Wq = jax.random.normal(ks[1], (HQ * D, HID), jnp.float32) * 0.02
        Wk = jax.random.normal(ks[2], (HK * D, HID), jnp.float32) * 0.02
        Wv = jax.random.normal(ks[3], (HK * D, HID), jnp.float32) * 0.02
        Wo = jax.random.normal(ks[4], (HID, HQ * D), jnp.float32) * 0.02
        q_norm_w = jax.random.uniform(ks[5], (D,), jnp.float32)
        k_norm_w = jax.random.uniform(ks[6], (D,), jnp.float32)
        k_cache = jax.random.normal(ks[7], (PAGES, PSIZE, HK, D), jnp.float32)
        v_cache = jax.random.normal(ks[8], (PAGES, PSIZE, HK, D), jnp.float32)
        block_table = jnp.arange(B * NPP, dtype=jnp.int32).reshape(B, NPP)
        cache_seqlens = jax.random.randint(ks[9], (B,), 0, 475).astype(jnp.int32)
        return dict(x=x, Wq=Wq, Wk=Wk, Wv=Wv, Wo=Wo, q_norm_w=q_norm_w, k_norm_w=k_norm_w, k_cache=k_cache, v_cache=v_cache, block_table=block_table, cache_seqlens=cache_seqlens)
    _L0_cond_all = _L0_cond_setup()
    _L0_cond_in = {k: v for k, v in _L0_cond_all.items() if k in ('Wq', 'Wk', 'Wv', 'Wo', 'q_norm_w', 'k_norm_w', 'k_cache', 'v_cache')}
    del _L0_cond_all

    def _L1_cond_setup():
        import jax, jax.numpy as jnp
        import numpy as np
        SESSION_CHANNELS = [128, 160, 192, 224, 240, 248, 252, 32]
        N_SESS = len(SESSION_CHANNELS)
        B, MAX_C, MAX_T = (16, 32, 512)
        HID, N_SRC = (64, 32)
        key = jax.random.key(seed)
        ks = jax.random.split(key, 7)
        session_ids = jax.random.randint(ks[0], (B,), 0, N_SESS)
        chan_table = jnp.asarray(SESSION_CHANNELS)
        channel_counts = chan_table[session_ids]
        seq_lens = jax.random.randint(ks[1], (B,), MAX_T // 2, MAX_T + 1)
        x = jax.random.normal(ks[2], (B, MAX_C, MAX_T), jnp.float32)
        cmask = (jnp.arange(MAX_C)[None, :] < channel_counts[:, None]).astype(x.dtype)
        tmask = (jnp.arange(MAX_T)[None, :] < seq_lens[:, None]).astype(x.dtype)
        x = x * cmask[:, :, None] * tmask[:, None, :]
        lim1 = 1.0 / np.sqrt(MAX_C)
        W_sess = jax.random.uniform(ks[3], (N_SESS, MAX_C, HID), jnp.float32, -lim1, lim1)
        b_sess = jax.random.uniform(ks[4], (N_SESS, HID), jnp.float32, -lim1, lim1)
        lim2 = 1.0 / np.sqrt(HID)
        W2 = jax.random.uniform(ks[5], (HID, N_SRC), jnp.float32, -lim2, lim2)
        b2 = jax.random.uniform(ks[6], (N_SRC,), jnp.float32, -lim2, lim2)
        return dict(x=x, session_ids=session_ids, channel_counts=channel_counts, seq_lens=seq_lens, W_sess=W_sess, b_sess=b_sess, W2=W2, b2=b2)
    _L1_cond_all = _L1_cond_setup()
    _L1_cond_in = {k: v for k, v in _L1_cond_all.items() if k in ('W_sess', 'b_sess', 'W2', 'b2')}
    del _L1_cond_all
    return {'x': x, 'itok_Bx16_0_63': itok_Bx16_0_63, 'itok_B_207_1644': itok_B_207_1644, 'itok_B_0_7': itok_B_0_7, 'itok_B_2182_4065': itok_B_2182_4065, '_lenS': _lenS, 'L0_cond_Wq': _L0_cond_in['Wq'], 'L0_cond_Wk': _L0_cond_in['Wk'], 'L0_cond_Wv': _L0_cond_in['Wv'], 'L0_cond_Wo': _L0_cond_in['Wo'], 'L0_cond_q_norm_w': _L0_cond_in['q_norm_w'], 'L0_cond_k_norm_w': _L0_cond_in['k_norm_w'], 'L0_cond_k_cache': _L0_cond_in['k_cache'], 'L0_cond_v_cache': _L0_cond_in['v_cache'], 'L1_cond_W_sess': _L1_cond_in['W_sess'], 'L1_cond_b_sess': _L1_cond_in['b_sess'], 'L1_cond_W2': _L1_cond_in['W2'], 'L1_cond_b2': _L1_cond_in['b2']}

def reference(x, itok_Bx16_0_63, itok_B_207_1644, itok_B_0_7, itok_B_2182_4065, _lenS, L0_cond_Wq, L0_cond_Wk, L0_cond_Wv, L0_cond_Wo, L0_cond_q_norm_w, L0_cond_k_norm_w, L0_cond_k_cache, L0_cond_v_cache, L1_cond_W_sess, L1_cond_b_sess, L1_cond_W2, L1_cond_b2):
    import jax
    import jax.numpy as jnp

    def _L0_cond_ref(x, Wq, Wk, Wv, Wo, q_norm_w, k_norm_w, k_cache, v_cache, block_table, cache_seqlens):
        import jax, jax.numpy as jnp
        import numpy as np
        B, S, HID = (4, 128, 512)
        D, HQ, HK = (128, 32, 8)
        PAGES, PSIZE, NPP = (64, 32, 16)
        THETA = 10000.0
        EPS = 1e-06
        SCALE = 1.0 / float(np.sqrt(D))

        def _rmsnorm(t, w):
            var = jnp.mean(t * t, axis=-1, keepdims=True)
            return t * jax.lax.rsqrt(var + EPS) * w

        def _rope(t, pos):
            inv_freq = 1.0 / THETA ** (jnp.arange(0, D, 2, dtype=jnp.float32) / D)
            freqs = pos[..., None].astype(jnp.float32) * inv_freq
            cos = jnp.cos(freqs)[:, :, None, :]
            sin = jnp.sin(freqs)[:, :, None, :]
            t1, t2 = (t[..., :D // 2], t[..., D // 2:])
            return jnp.concatenate([t1 * cos - t2 * sin, t2 * cos + t1 * sin], axis=-1)
        bsz, seqlen, _ = x.shape
        q = jnp.einsum('bsd,ed->bse', x, Wq).reshape(bsz, seqlen, HQ, D)
        k = jnp.einsum('bsd,ed->bse', x, Wk).reshape(bsz, seqlen, HK, D)
        v = jnp.einsum('bsd,ed->bse', x, Wv).reshape(bsz, seqlen, HK, D)
        q = _rmsnorm(q, q_norm_w)
        k = _rmsnorm(k, k_norm_w)
        pos = cache_seqlens[:, None] + jnp.arange(seqlen)[None, :]
        q = _rope(q, pos)
        k = _rope(k, pos)
        L = NPP * PSIZE
        kc = k_cache[block_table].reshape(bsz, L, HK, D)
        vc = v_cache[block_table].reshape(bsz, L, HK, D)
        k_all = jnp.concatenate([kc, k], axis=1)
        v_all = jnp.concatenate([vc, v], axis=1)
        valid_c = jnp.arange(L)[None, :] < cache_seqlens[:, None]
        valid = jnp.concatenate([valid_c, jnp.ones((bsz, seqlen), dtype=bool)], axis=1)
        rep = HQ // HK
        k_all = jnp.repeat(k_all, rep, axis=2)
        v_all = jnp.repeat(v_all, rep, axis=2)
        scores = jnp.einsum('bqhd,bkhd->bhqk', q, k_all) * SCALE
        scores = jnp.where(valid[:, None, None, :], scores, -1e+30)
        probs = jax.nn.softmax(scores, axis=-1)
        o = jnp.einsum('bhqk,bkhd->bqhd', probs, v_all)
        o = o.reshape(bsz, seqlen, HQ * D)
        return jnp.einsum('bse,de->bsd', o, Wo)

    def _L1_cond_ref(x, session_ids, channel_counts, seq_lens, W_sess, b_sess, W2, b2):
        import jax, jax.numpy as jnp
        import numpy as np
        SESSION_CHANNELS = [128, 160, 192, 224, 240, 248, 252, 32]
        N_SESS = len(SESSION_CHANNELS)
        B, MAX_C, MAX_T = (16, 32, 512)
        HID, N_SRC = (64, 32)
        cmask = (jnp.arange(x.shape[1])[None, :] < channel_counts[:, None]).astype(x.dtype)
        xm = x * cmask[:, :, None]
        W = W_sess[session_ids]
        b = b_sess[session_ids]
        h = jnp.einsum('bct,bch->bht', xm, W) + b[:, :, None]
        h = jax.nn.gelu(h, approximate=False)
        out = jnp.einsum('bht,hs->bst', h, W2) + b2[None, :, None]
        tmask = (jnp.arange(x.shape[2])[None, :] < seq_lens[:, None]).astype(x.dtype)
        return out * tmask[:, None, :]
    x = x + _L0_cond_ref(x, L0_cond_Wq, L0_cond_Wk, L0_cond_Wv, L0_cond_Wo, L0_cond_q_norm_w, L0_cond_k_norm_w, L0_cond_k_cache, L0_cond_v_cache, itok_Bx16_0_63, itok_B_207_1644)
    x = x + _L1_cond_ref(x, itok_B_0_7, _lenS, itok_B_2182_4065, L1_cond_W_sess, L1_cond_b_sess, L1_cond_W2, L1_cond_b2)
    return x

_drawn_inputs = setup_inputs


def setup_inputs(seed=0):
    import zlib

    import numpy as np

    out = dict(_drawn_inputs(seed))
    spreads = {}
    factors = {'L0_cond_Wk': 8.0,
     'L0_cond_Wv': 8.0,
     'L0_cond_k_norm_w': 8.0,
     'L0_cond_k_cache': 4.291,
     'L0_cond_v_cache': 3.106,
     'L1_cond_b_sess': 3.157}
    for name, (base, spread) in spreads.items():
        noise = np.random.default_rng([zlib.crc32(name.encode()), seed]).standard_normal(out[name].shape)
        drawn = base * np.exp(spread * noise) if base else spread * noise
        out[name] = jnp.asarray(drawn.astype(out[name].dtype))
    for name, factor in factors.items():
        out[name] = (out[name] * factor).astype(out[name].dtype)
    return out
```

```python
import math
from contextlib import ExitStack

import numpy as np
import concourse.bass as bass
from concourse import mybir

F32, F32R = mybir.dt.float32, mybir.dt.float32r
I32, U32 = mybir.dt.int32, mybir.dt.uint32
ALU = mybir.AluOpType
ACT = mybir.ActivationFunctionType

B, S, HID = 64, 32, 512
D, HQ, HK = 128, 32, 8
PAGES, PSIZE, NPP = 64, 32, 16
L = NPP * PSIZE
KEYS = L + S
P = 128
BT = P // S
NT = B // BT
NP = HK // 2
REP = HQ // HK
QH = 2 * REP
CH = HID // P
BLK = L // P
QC, KC, VC = QH * D, 2 * D, 2 * D
WC = QC + KC + VC
ROW = KC + VC
UN = 2 * BT
PU = UN * NT
SCALE = 1.0 / float(np.sqrt(D))
EPS = 1e-6
BIG = float(2.0 ** 101)
HALF = D // 2
N_SESS, MAX_C, HID1, N_SRC = 8, 32, 64, 32

TURN_PARTS = []
_left = 2 * math.pi
for _ in range(4):
    _unit = 2.0 ** (math.frexp(_left)[1] - 8)
    TURN_PARTS.append(math.floor(_left / _unit) * _unit)
    _left -= TURN_PARTS[-1]
TURN_PARTS.append(_left)
ROUND = 1.5 * 2.0 ** 23
PI_DOWN = 3.1415925

C_ID, C_RAMP, C_FREQ, C_IOTA = 0, P, P + L, P + L + HALF
C_TOK = P + 2 * L + HALF
C_HROW = C_TOK + 1
C_PAIR = C_HROW + 1
C_ALL = C_PAIR + NP


def cond_resid_kernel(nc, x, xT, wqkv, wo, norm_w, kv, table, lens, lens_b, sess_c, sess_h, chan, seq,
                      w_sess, b_sess, w2, b2, cst, out):
    ctx = ExitStack()
    with ctx:
        def sb(name, shape, dt=F32):
            return ctx.enter_context(nc.sbuf_tensor(name, shape, dt))

        def sem(name):
            return ctx.enter_context(nc.semaphore(name))

        WH, WL = sb("WH", [P, CH, WC], F32R), sb("WL", [P, CH, WC], F32R)
        WOH, WOL = sb("WOH", [P, QH, HID], F32R), sb("WOL", [P, QH, HID], F32R)
        XR = sb("XR", [P, CH, P])
        XH, XL = sb("XH", [P, CH, P], F32R), sb("XL", [P, CH, P], F32R)
        KV = sb("KV", [P, BT, BLK, ROW])
        KTH, KTL = sb("KTH", [P, 2, L], F32R), sb("KTL", [P, 2, L], F32R)
        PB = sb("PB", [P, 2, KEYS])
        PTS = sb("PTS", [P, 2, BLK, P])
        PN = sb("PN", [P, UN, P])
        O = sb("O", [P, 2, D])
        OTH, OTL = sb("OTH", [P, 2, QH, P], F32R), sb("OTL", [P, 2, QH, P], F32R)
        QTH = [sb(f"QTH{i}", [P, 2, BT, REP, S], F32R) for i in range(2)]
        QTL = [sb(f"QTL{i}", [P, 2, BT, REP, S], F32R) for i in range(2)]
        KNH, KNL = sb("KNH", [P, 2, 2, P], F32R), sb("KNL", [P, 2, 2, P], F32R)
        VN = sb("VN", [P, 2, VC])
        QU = sb("QU", [P, 2 * (QC + KC) + REP * D])
        QN, U, V = QU[:, 0:QC + KC], QU[:, QC + KC:2 * (QC + KC)], QU[:, 2 * (QC + KC):]
        MASK = sb("MASK", [P, 2, KEYS])
        ACC = sb("ACC", [P, 2, HID])
        TAB = sb("TAB", [P, 4, D])
        IDENT = sb("IDENT", [P, P])
        RAMP = sb("RAMP", [P, L])
        IDX = sb("IDX", [P, NT * BT * BLK], I32)
        IDXC = sb("IDXC", [P, 2, BT * BLK], U32)
        LENB = sb("LENB", [P, B])
        PAIR = sb("PAIR", [P, NP])
        BIAS, RSUM, RS = sb("BIAS", [P, UN]), sb("RSUM", [P, UN]), sb("RS", [P, UN])
        SS, RV, RSTD = (sb(n, [P, QH + 2]) for n in ("SS", "RV", "RSTD"))
        EXPO = sb("EXPO", [P, REP])
        ANG, TURNS, SIN = (QU[:, i * NT * HALF:(i + 1) * NT * HALF] for i in range(3))
        TABS = KV[:, :, :, :].rearrange("p b k (c d) -> p (b k) c d", d=D)
        NW = PTS[:, 0, 0:2, :]
        LENP = PTS[:, 1, 0, 0:NT]
        LENI = PTS[:, 1, 1, 0:NT].bitcast(I32)
        LENBI = PTS[:, 1, 2, 0:B].bitcast(I32)
        FREQ = PTS[:, 1, 3, 0:HALF]
        TOK2 = PTS[:, 1, 3, HALF:HALF + 2]
        TOK = TOK2[:, 0:1]

        KF = KV[:, :, :, :].rearrange("p b k c -> p (b k c)")
        X1 = KF[:, 0:1024].rearrange("p (i n) -> p i n", i=2)
        XM = KF[:, 1024:2048].rearrange("p (i n) -> p i n", i=2)
        HB = KF[:, 2048:4096].rearrange("p (i h n) -> p i h n", i=2, h=2)
        Y = KF[:, 4096:5120].rearrange("p (i n) -> p i n", i=2)
        Z = KF[:, 5120:6144].rearrange("p (i n) -> p i n", i=2)
        WS = KF[:, 6144:7168].rearrange("p (t n) -> p t n", t=NT)
        WB = KF[:, 7168:7680].rearrange("p (i h n) -> p i h n", i=2, h=2)
        W2B = QU[:, 0:256].rearrange("p (h n) -> p h n", h=2)
        IOTA = QU[:, 256:768]
        CM, SEQ, BS = QU[:, 768:784], QU[:, 784:800], QU[:, 800:832]
        CHANI, SEQI, SESSC, SESSH = (QU[:, a:b].bitcast(I32) for a, b in ((832, 848), (848, 864), (864, 880), (880, 912)))
        IDXW, IDXB = QU[:, 912:928].bitcast(U32), QU[:, 928:960].bitcast(U32)
        ROWS, B2C = QU[:, 960:962], QU[:, 962:963]
        L1_PAR = 2 + 5 * BT + 2

        def bank(name, shape):
            return ctx.enter_context(nc.psum_tensor(name, shape, F32))

        pS = bank("pS", [P, 1024])
        pKT, pPT, pO, pOT = (bank(n, [P, 512]) for n in ("pKT", "pPT", "pO", "pOT"))
        pF = [bank(f"pF{i}", [P, 512]) for i in range(2)]
        pPN = pO[0:S, P:2 * P]

        accd = nc.dram_tensor("accd", (NP + 1, NT, P, HID), F32, kind="Internal").ap()
        tabd = nc.dram_tensor("tabd", (NT, P, 4 * D), F32, kind="Internal").ap()

        d_cst, d_small, d_x0, d_tabs, d_tab, d_xr, d_acc, d_out = (
            sem("d_" + n) for n in ("cst", "small", "x0", "tabs", "tab", "xr", "acc", "out"))
        d_w = [sem(f"d_w{i}") for i in range(2)]
        d_kv = [sem(f"d_kv{i}") for i in range(BT)]
        t_s, t_kt, t_pt, t_pv, t_ot, t_qkv, t_op, t_qt = (sem("t_" + n) for n in ("s", "kt", "pt", "pv", "ot", "qkv", "op", "qt"))
        a_kth, a_pt, a_exp, a_oth, a_qkv, a_qth, a_xh, a_wh, a_sin = (
            sem("a_" + n) for n in ("kth", "pt", "exp", "oth", "qkv", "qth", "xh", "wh", "sin"))
        v_ktl, v_pn, v_max, v_otl, v_o, v_rs, v_ss, v_var, v_qn, v_v = (
            sem("v_" + n) for n in ("ktl", "pn", "max", "otl", "o", "rs", "ss", "var", "qn", "v"))
        v_qtl, v_xl, v_wl, v_op, v_mask, v_idx, v_angle, v_tabs, v_own = (
            sem("v_" + n) for n in ("qtl", "xl", "wl", "op", "mask", "idx", "angle", "tabs", "own"))
        g_rstd, g_u, g_rope = (sem("g_" + n) for n in ("rstd", "u", "rope"))
        v_step, g_step, s_step = (sem(n) for n in ("v_step", "g_step", "s_step"))
        CRED = UN
        e_par, e_w, e_b = (sem("e_" + n) for n in ("par", "w", "b"))
        e_x = [sem(f"e_x{i}") for i in range(2)]
        e_out = [sem(f"e_out{i}") for i in range(2)]
        f_zero, f_idx, f_w, f_xm, f_h, f_gelu, f_y, f_yb, f_m, f_z, f_chan = (
            sem("f_" + n) for n in ("zero", "idx", "w", "xm", "h", "gelu", "y", "yb", "m", "z", "chan"))

        block = ctx.enter_context(nc.Block())

        def pairs(e, before, tile, after):
            with e.Fori(0, NP) as p:
                T0 = p * NT
                before(p, T0)
                tile(p, T0, 0, 0, first=True, ahead=2)
                with e.Fori(0, (NT - 4) // 2) as i:
                    tile(p, T0 + i * 2 + 1, i * 2 + 1, 1, first=False, ahead=2)
                    tile(p, T0 + i * 2 + 2, i * 2 + 2, 0, first=False, ahead=2)
                tile(p, T0 + NT - 3, NT - 3, 1, first=False, ahead=2)
                tile(p, T0 + NT - 2, NT - 2, 0, first=False, ahead=1)
                tile(p, T0 + NT - 1, NT - 1, 1, first=False, ahead=0)
                after(p, T0 + NT)

        def done(T, u):
            return T * UN + (u + 1)

        def third(j):
            h0, n = ((0, REP), (REP, REP), (2 * REP, 2))[j]
            return h0, n, slice(h0 * D, (h0 + n) * D)

        def by_head(ap, n):
            return ap.rearrange("p (h d) -> p h d", h=n)

        def o_turned(dst, u, par):
            b, hk = divmod(u, 2)
            return dst[:, par, hk * REP:(hk + 1) * REP, b * S:(b + 1) * S]

        def q_turned(q, kn, j, par):
            if j == 2:
                return kn[:, par, :, :]
            return q[par][:, j, :, :, :].rearrange("p b h s -> p h b s")

        def f_turned(j):
            n = third(j)[1]
            if j == 2:
                return pF[0][:, 0:2 * P].rearrange("p (h n) -> p h n", h=2)
            return pF[j % 2][:, 0:n * P].rearrange("p (h b s) -> p h b s", h=n, b=BT)

        @block.sync
        def _(sp):
            sp.dma_start(IDENT[:, :], cst[:, C_ID:C_ID + P]).then_inc(d_cst, 16)
            sp.dma_start(RAMP[:, :], cst[:, C_RAMP:C_RAMP + L]).then_inc(d_cst, 16)
            sp.dma_start(PAIR[:, :], cst[:, C_PAIR:C_PAIR + NP]).then_inc(d_cst, 16)
            sp.dma_start(FREQ, cst[:, C_FREQ:C_FREQ + HALF]).then_inc(d_small, 16)
            sp.dma_start(TOK2, cst[:, C_TOK:C_TOK + 2]).then_inc(d_small, 16)
            sp.dma_start(NW, norm_w.partition_broadcast(P)).then_inc(d_small, 16)
            for b in range(BT):
                sp.dma_start(LENI[b * S:(b + 1) * S, :], lens_b[b, :].partition_broadcast(S)).then_inc(d_small, 16)
                sp.dma_start(IDX[b * S:(b + 1) * S, :], table[b, :].partition_broadcast(S)).then_inc(d_small, 16)
            sp.dma_start(LENBI, lens.partition_broadcast(P)).then_inc(d_small, 16)
            sp.dma_start(accd[0].rearrange("t p n -> (t p) n"), x).then_inc(d_x0, 16)
            sp.wait_ge(v_tabs, 1)
            sp.dma_start(tabd.rearrange("t p n -> p t n"), TABS.rearrange("p t c d -> p t (c d)")).then_inc(d_tabs, 16)
            sp.wait_ge(d_tabs, 16)
            sp.wait_ge(d_x0, 16)

            def load_tab(t):
                sp.dma_start(TAB[:, :, :], tabd[bass.ds(t, 1)].rearrange("a p (c d) -> p (a c) d", d=D)).then_inc(d_tab, 16)

            def load_x(t):
                sp.dma_start(XR[:, :, :], xT[bass.ds(t, 1)].rearrange("a p c n -> p (a c) n")).then_inc(d_xr, 16)

            def acc_in(p, t, par):
                sp.dma_start(ACC[:, par, :], accd[bass.ds(p, 1), bass.ds(t, 1)].rearrange("a b p n -> p (a b n)"))\
                    .then_inc(d_acc, 16)

            def acc_out(p, T, t, par):
                sp.wait_ge(v_op, T + 2)
                sp.dma_start(accd[bass.ds(p + 1, 1), bass.ds(t, 1)].rearrange("a b p n -> p (a b n)"), ACC[:, par, :])\
                    .then_inc(d_out, 16)
                sp.wait_ge(d_out, (T + 1) * 16)
                sp.sem_inc(s_step, 1)

            def before(p, T):
                sp.wait_ge(v_op, T + 1)
                for c in range(2 * CH):
                    if c >= 2:
                        sp.wait_ge(v_wl, p * (2 * CH) + (c - 1))
                    if c < CH:
                        src = wqkv[bass.ds(p, 1), :, c, :].rearrange("a p n -> p (a n)")
                        sp.dma_start(QU[:, (c % 2) * WC:(c % 2 + 1) * WC], src).then_inc(d_w[c % 2], 16)
                    else:
                        src = wo[bass.ds(p, 1), :, 2 * (c - CH):2 * (c - CH) + 2, :].rearrange("a p h n -> p (a h n)")
                        sp.dma_start(QU[:, (c % 2) * WC:(c % 2) * WC + 2 * HID], src).then_inc(d_w[c % 2], 16)
                    if c == 1:
                        load_x(0)
                load_tab(0)
                sp.wait_ge(v_xl, T + 1)
                load_x(1)

            def tile(p, T, t, par, first, ahead):
                if ahead >= 1:
                    sp.wait_ge(g_rope, T * 3 + 3)
                    load_tab(t + 1)
                if not first:
                    acc_in(p, t - 1, 1 - par)
                if ahead >= 2:
                    sp.wait_ge(v_xl, T + 2)
                    load_x(t + 2)
                if not first:
                    acc_out(p, T - 1, t - 1, 1 - par)

            def after(p, T):
                acc_in(p, NT - 1, 1)
                acc_out(p, T - 1, NT - 1, 1)

            pairs(sp, before, tile, after)

            sp.wait_ge(f_zero, 1)
            sp.dma_start(IOTA, cst[:, C_IOTA:C_IOTA + L]).then_inc(e_par, 16)
            sp.dma_start(ROWS, cst[:, C_TOK:C_TOK + 2]).then_inc(e_par, 16)
            for b in range(BT):
                rows = slice(b * S, (b + 1) * S)
                sp.dma_start(CHANI[rows, :], chan[b, :].partition_broadcast(S)).then_inc(e_par, 16)
                sp.dma_start(SEQI[rows, :], seq[b, :].partition_broadcast(S)).then_inc(e_par, 16)
                sp.dma_start(SESSC[rows, :], sess_c[b, :].partition_broadcast(S)).then_inc(e_par, 16)
                sp.dma_start(B2C[rows, :], b2, allow_slow_non_contiguous=True).then_inc(e_par, 16)
                half, odd = divmod(b, 2)
                sp.dma_start(W2B[odd * HID1:(odd + 1) * HID1, half, b * N_SRC:(b + 1) * N_SRC], w2).then_inc(e_par, 16)
            for odd in range(2):
                sp.dma_start(SESSH[odd * HID1:(odd + 1) * HID1, :], sess_h[odd, :].partition_broadcast(HID1)).then_inc(e_par, 16)

            def l1_tile(t, par, first):
                if not first:
                    sp.wait_ge(f_z, t - 1)
                sp.dma_start(X1[:, par, :], accd[NP, bass.ds(t, 1)].rearrange("a p n -> p (a n)")).then_inc(e_x[par], 16)

            def l1_out(t, par):
                sp.wait_ge(f_z, t + 1)
                sp.dma_start(out[bass.ds(t, 1)].rearrange("a p n -> p (a n)"), Z[:, par, :]).then_inc(e_out[par], 16)

            l1_tile(0, 0, True)
            l1_tile(1, 1, True)
            with sp.Fori(0, NT // 2 - 1) as i:
                for par in range(2):
                    l1_out(i * 2 + par, par)
                    l1_tile(i * 2 + (2 + par), par, False)
            for par in range(2):
                l1_out(NT - 2 + par, par)
            for par in range(2):
                sp.wait_ge(e_out[par], NT // 2 * 16)

        @block.gpsimd
        def _(pool):
            def load_kv(T, par, b):
                pool.wait_ge(v_idx, T + 1)
                pool.wait_ge(t_pv, done(T, 2 * b + 1))
                pool.sem_inc(g_step, 1)
                for blk in range(BLK):
                    n = b * BLK + blk
                    nc.gpsimd.indirect_dma_start(
                        out=KV[:, b, blk, :], out_offset=None, in_=kv,
                        in_offset=bass.IndirectOffsetOnAxis(ap=IDXC[:, par, n:n + 1], axis=0)).then_inc(d_kv[b], 16)

            def rsqrt(T, j):
                h0, n, _ = third(j)
                pool.wait_ge(v_var, T * 3 + (j + 1))
                nc.gpsimd.tensor_tensor(RSTD[:, h0:h0 + n], RV[:, h0:h0 + n], EXPO[:, 0:n], ALU.pow).then_inc(g_rstd, 1)

            def rope(T, j):
                _, n, cols = third(j)
                u = by_head(U[:, cols], n)
                c = TAB[:, 0 if j < 2 else 2, :].unsqueeze(1).to_broadcast([P, n, D])
                pool.wait_ge(d_tab, (T + 1) * 16)
                pool.wait_ge(v_qn, T * 3 + (j + 1))
                nc.gpsimd.tensor_tensor(u, by_head(QN[:, cols], n), c, ALU.mult).then_inc(g_u, 1)
                pool.wait_ge(g_u, T * 3 + (j + 1))
                pool.wait_ge(v_v, T * 3 + (j + 1))
                v = by_head(V[:, 0:n * D], n)
                nc.gpsimd.tensor_tensor(u[:, :, 0:HALF], u[:, :, 0:HALF], v[:, :, HALF:D], ALU.add)
                nc.gpsimd.tensor_tensor(u[:, :, HALF:D], u[:, :, HALF:D], v[:, :, 0:HALF], ALU.add).then_inc(g_rope, 1)

            def before(p, T):
                load_kv(T, 0, 0)
                load_kv(T, 0, 1)
                for j in range(3):
                    rsqrt(T, j)
                    rope(T, j)

            def tile(p, T, t, par, first, ahead):
                load_kv(T, par, 2)
                for u in range(1, UN):
                    if u == 2:
                        load_kv(T, par, 3)
                    if ahead and u in (2, 3, 4):
                        rope(T + 1, u - 2)
                    if ahead and u in (1, 2, 3):
                        rsqrt(T + 1, u - 1)
                    if ahead and u in (4, 6):
                        load_kv(T + 1, 1 - par, u // 2 - 2)

            pool.wait_ge(d_tabs, 16)
            pairs(pool, before, tile, lambda p, T: None)

            pool.wait_ge(f_idx, 2)
            for t in range(NT):
                nc.gpsimd.indirect_dma_start(out=WS[:, t, :], out_offset=None, in_=w_sess,
                                             in_offset=bass.IndirectOffsetOnAxis(ap=IDXW[:, t:t + 1], axis=0)).then_inc(e_w, 16)
                for half in range(2):
                    n = 2 * t + half
                    nc.gpsimd.indirect_dma_start(out=BS[:, n:n + 1], out_offset=None, in_=b_sess,
                                                 in_offset=bass.IndirectOffsetOnAxis(ap=IDXB[:, n:n + 1], axis=0)).then_inc(e_b, 16)

        @block.scalar
        def _(act):
            def copy(dst, src):
                return nc.scalar.activation(dst, src, ACT.Copy)

            act.wait_ge(v_angle, 1)
            nc.scalar.activation(SIN, ANG, ACT.Sin).then_inc(a_sin, 1)
            act.wait_ge(v_angle, 2)
            nc.scalar.activation(TURNS, TURNS, ACT.Sin).then_inc(a_sin, 1)

            def oth(T, u, par):
                act.wait_ge(t_ot, done(T, u))
                copy(o_turned(OTH, u % UN, par if u >= 0 else 1 - par),
                     pOT[:, 0:P].rearrange("p (h s) -> p h s", h=REP)).then_inc(a_oth, 1)

            def kth(T, u):
                act.wait_ge(t_kt, done(T, u))
                copy(KTH[:, u % 2, :], pKT[:, :]).then_inc(a_kth, 1)

            def pt(T, u):
                act.wait_ge(t_pt, done(T, u))
                copy(PTS[:, u % 2, :, :].rearrange("p k n -> p (k n)"), pPT[:, :]).then_inc(a_pt, 1)

            def exp(T, u):
                act.wait_ge(v_max, done(T, u))
                nc.scalar.activation(PB[:, u % 2, :], PB[:, u % 2, :], ACT.Exp, bias=BIAS[:, u:u + 1], scale=-1.0,
                                     accum_out=RSUM[:, u:u + 1]).then_inc(a_exp, 1)

            def projected(T, j, par):
                act.wait_ge(t_qkv, T * 3 + (j + 1))
                _, n, cols = third(j)
                ev = copy(QN[:, cols], pF[j % 2][:, 0:n * D])
                if j == 2:
                    ev = copy(VN[:, par, :], pF[0][:, KC:KC + VC])
                ev.then_inc(a_qkv, 1)

            def qth(T, j, par):
                act.wait_ge(t_qt, T * 3 + (j + 1))
                copy(q_turned(QTH, KNH, j, par), f_turned(j)).then_inc(a_qth, 1)

            def xh(T):
                act.wait_ge(d_xr, (T + 1) * 16)
                copy(XH[:, :, :], XR[:, :, :]).then_inc(a_xh, 1)

            def before(p, T):
                for c in range(2 * CH):
                    act.wait_ge(d_w[c % 2], (p * CH + (c // 2 + 1)) * 16)
                    w = QU[:, (c % 2) * WC:]
                    if c < CH:
                        copy(WH[:, c, :], w[:, 0:WC]).then_inc(a_wh, 1)
                    else:
                        h = 2 * (c - CH)
                        copy(WOH[:, h:h + 2, :].rearrange("p h n -> p (h n)"), w[:, 0:2 * HID]).then_inc(a_wh, 1)
                xh(T)
                for j in range(3):
                    projected(T, j, 0)
                xh(T + 1)
                kth(T, 0)
                for j in range(3):
                    qth(T, j, 0)

            def tile(p, T, t, par, first, ahead):
                for u in range(UN):
                    if not (first and u < 3):
                        oth(T, u - 3, par)
                    if ahead or u < UN - 1:
                        kth(T, u + 1)
                    if not (first and u < 1):
                        pt(T, u - 1)
                    exp(T, u)
                    if ahead and u < 3:
                        projected(T + 1, u, 1 - par)
                    if ahead >= 2 and u == 4:
                        act.wait_ge(t_qkv, T * 3 + 6)
                        xh(T + 2)
                    if ahead and u == 6:
                        qth(T + 1, 0, 1 - par)
                        qth(T + 1, 1, 1 - par)
                    if ahead and u == 7:
                        qth(T + 1, 2, 1 - par)

            def after(p, T):
                for u in range(3):
                    oth(T, u - 3, 0)
                    if u == 0:
                        pt(T, -1)

            pairs(act, before, tile, after)

            act.wait_ge(e_b, 2 * NT * 16)
            act.wait_ge(e_par, L1_PAR * 16)

            def l1_gelu(t, par, half):
                act.wait_ge(f_h, t * 2 + (half + 1))
                nc.scalar.activation(HB[:, par, half, :], pS[:, half * HID:(half + 1) * HID], ACT.Gelu,
                                     bias=BS[:, bass.ds(t * 2 + half, 1)]).then_inc(f_gelu, 1)

            def l1_tile(t, par):
                for half in range(2):
                    l1_gelu(t, par, half)
                act.wait_ge(f_y, t + 1)
                nc.scalar.activation(Y[:, par, :], pKT[:, :], ACT.Identity, bias=B2C[:, 0:1]).then_inc(f_yb, 1)

            with act.Fori(0, NT // 2) as i:
                for par in range(2):
                    l1_tile(i * 2 + par, par)

        @block.vector
        def _(dve):
            chain = [0]

            def link(ins):
                chain[0] += 1
                ins.then_inc(v_own, 1)
                dve.wait_ge(v_own, chain[0])

            def minus(dst, a, hi):
                return nc.vector.tensor_tensor(dst, a, hi.bitcast(F32), ALU.subtract)

            link(nc.vector.memset(PN[:, :, :], 0.0))
            link(nc.vector.memset(MASK[:, :, L:KEYS], 0.0))
            link(nc.vector.memset(EXPO[:, :], -0.5))
            dve.sem_inc(v_op, 1)
            dve.wait_ge(d_small, (4 + 2 * BT) * 16)
            dve.wait_ge(d_cst, 3 * 16)
            link(nc.vector.tensor_scalar(IDX[:, :], IDX[:, :], float(PSIZE), TOK, ALU.mult, ALU.add))
            link(nc.vector.tensor_scalar(LENB[:, :], LENBI, BIG, None, ALU.mult))
            link(nc.vector.tensor_scalar(LENP, LENI, TOK, None, ALU.add))
            ang3 = ANG.rearrange("p (t f) -> p t f", t=NT)
            link(nc.vector.tensor_tensor(ang3, LENP.unsqueeze(2).to_broadcast([P, NT, HALF]),
                                         FREQ.unsqueeze(1).to_broadcast([P, NT, HALF]), ALU.mult))
            link(nc.vector.tensor_scalar(TURNS, ANG, 1.0 / (2 * math.pi), None, ALU.mult))
            link(nc.vector.tensor_scalar(TURNS, TURNS, ROUND, None, ALU.add))
            link(nc.vector.tensor_scalar(TURNS, TURNS, -ROUND, None, ALU.add))
            for part in TURN_PARTS:
                link(nc.vector.scalar_tensor_tensor(out=ANG, in0=TURNS, scalar=-part, in1=ANG, op0=ALU.mult, op1=ALU.add))
            link(nc.vector.tensor_scalar(ANG, ANG, PI_DOWN, -PI_DOWN, ALU.min, ALU.max))
            dve.sem_inc(v_angle, 1)
            link(nc.vector.scalar_tensor_tensor(out=TURNS, in0=ANG, scalar=-1.0, in1=ANG, op0=ALU.mult, op1=ALU.max))
            link(nc.vector.tensor_scalar(TURNS, TURNS, -1.0, math.pi / 2, ALU.mult, ALU.add))
            dve.sem_inc(v_angle, 1)
            dve.wait_ge(a_sin, 2)
            cos3, sin3 = (a.rearrange("p (t f) -> p t f", t=NT) for a in (TURNS, SIN))
            for w in range(2):
                for half in range(2):
                    cols = slice(half * HALF, (half + 1) * HALF)
                    wt = NW[:, w, cols].unsqueeze(1).to_broadcast([P, NT, HALF])
                    nc.vector.tensor_tensor(TABS[:, :, 2 * w, cols], cos3, wt, ALU.mult)
                    last = nc.vector.scalar_tensor_tensor(out=TABS[:, :, 2 * w + 1, cols], in0=sin3, scalar=1.0 - 2.0 * half,
                                                          in1=wt, op0=ALU.mult, op1=ALU.mult)
            last.then_inc(v_tabs, 1)

            def mask(T, t, b):
                nc.vector.tensor_scalar(MASK[:, b % 2, 0:L], RAMP[:, :], LENB[:, bass.ds(t * BT + b, 1)], 0.0,
                                        ALU.add, ALU.min).then_inc(v_mask, 1)

            def rows(p, t, par):
                nc.vector.tensor_scalar(IDXC[:, par, :], IDX[:, bass.ds(t * (BT * BLK), BT * BLK)],
                                        PAIR[:, bass.ds(p, 1)], None, ALU.add).then_inc(v_idx, 1)

            def o(T, u):
                dve.wait_ge(t_pv, done(T, u) + CRED)
                dve.wait_ge(v_rs, done(T, u))
                nc.vector.tensor_scalar(O[:, u % 2, :], pO[:, 0:D], RS[:, u % UN:u % UN + 1], None, ALU.mult).then_inc(v_o, 1)

            def masked(T, u):
                dve.wait_ge(t_s, done(T, u))
                dve.wait_ge(v_mask, T * BT + (u // 2 + 1))
                dve.sem_inc(v_step, 1)
                nc.vector.tensor_tensor_reduce(out=PB[:, u % 2, :], in0=pS[:, 0:KEYS], in1=MASK[:, u // 2 % 2, :],
                                               scale=-SCALE, scalar=3e38, op0=ALU.add, op1=ALU.min,
                                               accum_out=BIAS[:, u:u + 1]).then_inc(v_max, 1)

            def otl(T, u, par):
                dve.wait_ge(a_oth, done(T, u))
                par = par if u >= 0 else 1 - par
                minus(o_turned(OTL, u % UN, par), pOT[:, 0:P].rearrange("p (h s) -> p h s", h=REP),
                      o_turned(OTH, u % UN, par)).then_inc(v_otl, 1)

            def ktl(T, u):
                dve.wait_ge(a_kth, done(T, u))
                minus(KTL[:, u % 2, :], pKT[:, :], KTH[:, u % 2, :]).then_inc(v_ktl, 1)

            def rs(T, u):
                dve.wait_ge(a_exp, done(T, u))
                u %= UN
                nc.vector.reciprocal(RS[:, u:u + 1], RSUM[:, u:u + 1]).then_inc(v_rs, 1)

            def pn(T, u):
                dve.wait_ge(t_pt, done(T, u))
                u %= UN
                b = u // 2
                nc.vector.tensor_copy(PN[b * S:(b + 1) * S, u, :], pPN).then_inc(v_pn, 1)

            def squares(T, j):
                h0, n, _ = third(j)
                dve.wait_ge(a_qkv, T * 3 + (j + 1))
                for h in range(h0, h0 + n):
                    q = QN[:, h * D:(h + 1) * D]
                    last = nc.vector.tensor_tensor_reduce(out=U[:, h * D:(h + 1) * D], in0=q, in1=q, scale=1.0, scalar=0.0,
                                                          op0=ALU.mult, op1=ALU.add, accum_out=SS[:, h:h + 1])
                last.then_inc(v_ss, 1)
                dve.wait_ge(v_ss, T * 3 + (j + 1))
                nc.vector.tensor_scalar(RV[:, h0:h0 + n], SS[:, h0:h0 + n], 1.0 / D, EPS, ALU.mult, ALU.add).then_inc(v_var, 1)

            def normalise(T, j):
                h0, n, cols = third(j)
                dve.wait_ge(g_rstd, T * 3 + (j + 1))
                q = by_head(QN[:, cols], n)
                nc.vector.tensor_tensor(q, q, RSTD[:, h0:h0 + n].unsqueeze(2).to_broadcast([P, n, D]), ALU.mult).then_inc(v_qn, 1)
                dve.wait_ge(v_qn, T * 3 + (j + 1))
                dve.wait_ge(d_tab, (T + 1) * 16)
                if j:
                    dve.wait_ge(g_rope, T * 3 + j)
                s = TAB[:, 1 if j < 2 else 3, :].unsqueeze(1).to_broadcast([P, n, D])
                nc.vector.tensor_tensor(by_head(V[:, 0:n * D], n), q, s, ALU.mult).then_inc(v_v, 1)

            def qtl(T, j, par):
                dve.wait_ge(a_qth, T * 3 + (j + 1))
                minus(q_turned(QTL, KNL, j, par), f_turned(j), q_turned(QTH, KNH, j, par)).then_inc(v_qtl, 1)

            def xl(T):
                dve.wait_ge(a_xh, T + 1)
                minus(XL[:, :, :], XR[:, :, :], XH[:, :, :]).then_inc(v_xl, 1)

            def add(T, par):
                dve.wait_ge(d_acc, (T + 1) * 16)
                dve.wait_ge(t_op, T + 1)
                nc.vector.tensor_tensor(ACC[:, par, :], pF[1][:, :], ACC[:, par, :], ALU.add).then_inc(v_op, 1)

            def before(p, T):
                rows(p, 0, 0)
                mask(T, 0, 0)
                for c in range(2 * CH):
                    dve.wait_ge(a_wh, p * (2 * CH) + (c + 1))
                    w = QU[:, (c % 2) * WC:]
                    if c < CH:
                        minus(WL[:, c, :], w[:, 0:WC], WH[:, c, :]).then_inc(v_wl, 1)
                    else:
                        h = slice(2 * (c - CH), 2 * (c - CH) + 2)
                        minus(WOL[:, h, :].rearrange("p h n -> p (h n)"), w[:, 0:2 * HID],
                              WOH[:, h, :].rearrange("p h n -> p (h n)")).then_inc(v_wl, 1)
                xl(T)
                for j in range(3):
                    squares(T, j)
                    normalise(T, j)
                xl(T + 1)
                ktl(T, 0)
                for j in range(3):
                    qtl(T, j, 0)

            def tile(p, T, t, par, first, ahead):
                for u in range(UN):
                    if not (first and u < 3):
                        o(T, u - 3)
                    masked(T, u)
                    if not (first and u < 3):
                        otl(T, u - 3, par)
                    if ahead or u < UN - 1:
                        ktl(T, u + 1)
                    if not (first and u < 1):
                        rs(T, u - 1)
                        pn(T, u - 1)
                    if u % 2 and (ahead or u < UN - 1):
                        mask(T, t, u // 2 + 1)
                    if ahead and u in (2, 3, 4):
                        normalise(T + 1, u - 2)
                    if ahead and u in (1, 2, 3):
                        squares(T + 1, u - 1)
                    if ahead and u == 3:
                        rows(p, t + 1, 1 - par)
                    if ahead >= 2 and u == 4:
                        xl(T + 2)
                    if not first and u == 5:
                        add(T - 1, 1 - par)
                    if ahead and u == 6:
                        qtl(T + 1, 0, 1 - par)
                        qtl(T + 1, 1, 1 - par)
                    if ahead and u == 7:
                        qtl(T + 1, 2, 1 - par)

            def after(p, T):
                for u in range(3):
                    o(T, u - 3)
                    otl(T, u - 3, 0)
                    if u == 0:
                        rs(T, -1)
                        pn(T, -1)
                add(T - 1, 1)

            pairs(dve, before, tile, after)

            dve.wait_ge(d_out, NP * NT * 16)
            link(nc.vector.memset(W2B[:, :, :], 0.0))
            link(nc.vector.memset(WB[:, :, :, :], 0.0))
            dve.sem_inc(f_zero, 1)
            dve.wait_ge(e_par, L1_PAR * 16)
            nc.vector.tensor_scalar(IDXW, SESSC, float(MAX_C), ROWS[:, 0:1], ALU.mult, ALU.add).then_inc(f_idx, 1)
            nc.vector.tensor_scalar(IDXB, SESSH, float(HID1), ROWS[:, 1:2], ALU.mult, ALU.add).then_inc(f_idx, 1)
            link(nc.vector.tensor_scalar(CM, CHANI, ROWS[:, 0:1], None, ALU.is_gt))
            link(nc.vector.tensor_copy(SEQ, SEQI))
            dve.wait_ge(e_w, NT * 16)

            def l1_in(t, par, first):
                n = slice(0, HID1)
                if not first:
                    dve.wait_ge(f_h, t * 2 - 2)
                for b in range(BT):
                    half, odd = divmod(b, 2)
                    nc.vector.tensor_copy(WB[b * S:(b + 1) * S, par, half, odd * HID1:(odd + 1) * HID1],
                                          WS[b * S:(b + 1) * S, bass.ds(t, 1), n].rearrange("p a n -> p (a n)"))
                dve.wait_ge(e_x[par], (t // 2 + 1) * 16 if isinstance(t, int) else (t - par) * 8 + 16)
                nc.vector.tensor_scalar(XM[:, par, :], X1[:, par, :], CM[:, bass.ds(t, 1)], None, ALU.mult).then_inc(f_xm, 1)

            def l1_out(t, par, first):
                dve.wait_ge(f_yb, t + 1)
                nc.vector.scalar_tensor_tensor(out=Y[:, par, :], in0=IOTA, scalar=SEQ[:, bass.ds(t, 1)], in1=Y[:, par, :],
                                               op0=ALU.is_lt, op1=ALU.mult).then_inc(f_m, 1)
                dve.wait_ge(f_m, t + 1)
                if not first:
                    dve.wait_ge(e_out[par], (t - par) * 8)
                nc.vector.tensor_tensor(Z[:, par, :], Y[:, par, :], X1[:, par, :], ALU.add).then_inc(f_z, 1)

            l1_in(0, 0, True)
            l1_in(1, 1, True)
            for par in range(2):
                l1_out(par, par, True)
                l1_in(2 + par, par, False)
            with dve.Fori(1, NT // 2 - 1) as i:
                for par in range(2):
                    l1_out(i * 2 + par, par, False)
                    l1_in(i * 2 + (2 + par), par, False)
            for par in range(2):
                l1_out(NT - 2 + par, par, False)

        @block.tensor
        def _(pe):
            mm, turn = nc.tensor.matmul, nc.tensor.transpose
            pe.sem_inc(t_pv, CRED)
            pe.wait_ge(d_cst, 3 * 16)

            def product(dst, terms):
                n = 3 * len(terms)
                steps = [x for lh, ll, rh, rl in terms for x in ((lh, rh), (lh, rl), (ll, rh))]
                for i, (a, b) in enumerate(steps):
                    last = mm(dst, a, b, start=(i == 0), stop=(i == n - 1))
                return last

            def qkv(T, j):
                _, n, cols = third(j)
                if j == 2:
                    cols = slice(cols.start, WC)
                    pe.wait_ge(a_qkv, T * 3 + 1)
                product(pF[j % 2][:, 0:cols.stop - cols.start],
                        [(XH[:, c, :], XL[:, c, :], WH[:, c, cols], WL[:, c, cols]) for c in range(CH)]).then_inc(t_qkv, 1)

            def qt(T, j):
                h0, n, _ = third(j)
                pe.wait_ge(g_rope, T * 3 + (j + 1))
                if j == 0:
                    pe.wait_ge(a_qkv, T * 3 + 3)
                if j == 2:
                    pe.wait_ge(v_qtl, T * 3 + 1)
                for h in range(n):
                    last = turn(pF[j % 2][:, h * P:(h + 1) * P], U[:, (h0 + h) * D:(h0 + h + 1) * D], IDENT[:, :])
                last.then_inc(t_qt, 1)

            def scores(T, u, par):
                b, hk = divmod(u, 2)
                pe.wait_ge(v_ktl, done(T, u))
                qh, ql = (q[par][:, hk, b, :, :].rearrange("p h s -> p (h s)") for q in (QTH, QTL))
                new = slice(b * S, (b + 1) * S)
                product(pS[:, 0:L], [(qh, ql, KTH[:, u % 2, :], KTL[:, u % 2, :])])
                product(pS[:, L:KEYS], [(qh, ql, KNH[:, par, hk, new], KNL[:, par, hk, new])]).then_inc(t_s, 1)

            def ot(T, u, wait_bank):
                pe.wait_ge(v_o, done(T, u))
                if wait_bank:
                    pe.wait_ge(v_otl, done(T, u - 1))
                turn(pOT[:, 0:P], O[:, u % 2, :], IDENT[:, :]).then_inc(t_ot, 1)

            def kt(T, u, new_batch):
                b, hk = divmod(u % UN, 2)
                if new_batch:
                    pe.wait_ge(d_kv[b], (T + (1 + u // UN)) * (16 * BLK))
                for k in range(BLK):
                    last = turn(pKT[:, k * P:(k + 1) * P], KV[:, b, k, hk * D:(hk + 1) * D], IDENT[:, :])
                last.then_inc(t_kt, 1)

            def pt(T, u, wait_bank):
                pe.wait_ge(a_exp, done(T, u))
                if wait_bank:
                    pe.wait_ge(a_pt, done(T, u - 1))
                    pe.wait_ge(v_pn, done(T, u - 1))
                for k in range(BLK):
                    turn(pPT[:, k * P:(k + 1) * P], PB[:, u % 2, k * P:(k + 1) * P], IDENT[:, :])
                turn(pPN, PB[:, u % 2, L:KEYS], IDENT[:, :]).then_inc(t_pt, 1)

            def pv(T, u, par, ahead):
                pe.wait_ge(a_pt, done(T, u))
                pe.wait_ge(v_pn, done(T, u + ahead))
                par = par if u >= 0 else 1 - par
                u %= UN
                b, hk = divmod(u, 2)
                for k in range(BLK):
                    mm(pO[:, 0:D], PTS[:, u % 2, k, :], KV[:, b, k, KC + hk * D:KC + (hk + 1) * D], start=(k == 0), stop=False)
                mm(pO[:, 0:D], PN[:, u, :], VN[:, par, hk * D:(hk + 1) * D], start=False, stop=True).then_inc(t_pv, 1)

            def op(T, heads, par):
                for h in heads:
                    for i, (a, b) in enumerate(((OTH, WOH), (OTH, WOL), (OTL, WOH))):
                        last = mm(pF[1][:, :], a[:, par, h, :], b[:, h, :], start=(h == 0 and i == 0),
                                  stop=(h == QH - 1 and i == 2))
                if heads.stop == QH:
                    last.then_inc(t_op, 1)

            def before(p, T):
                pe.wait_ge(v_op, T + 1)
                pe.wait_ge(v_wl, p * (2 * CH) + 2 * CH)
                pe.wait_ge(v_xl, T + 1)
                for j in range(3):
                    qkv(T, j)
                kt(T, 0, True)
                for j in range(3):
                    qt(T, j)

            def tile(p, T, t, par, first, ahead):
                pe.wait_ge(v_qtl, T * 3 + 3)
                for u in range(UN):
                    if not (first and u == 0):
                        pe.wait_ge(v_max, done(T, u - 1))
                    scores(T, u, par)
                    if not (first and u < 3):
                        ot(T, u - 3, not (first and u == 3))
                    if ahead or u < UN - 1:
                        kt(T, u + 1, u % 2 == 1)
                    if not (first and u < 1):
                        pt(T, u - 1, not (first and u == 1))
                    if ahead and u < 3:
                        if u == 0:
                            pe.wait_ge(v_xl, T + 2)
                        qkv(T + 1, u)
                    if not first and 3 <= u < 6:
                        if u == 3:
                            pe.wait_ge(v_otl, T * UN)
                            if ahead:
                                pe.wait_ge(a_qkv, T * 3 + 5)
                        op(T - 1, range((u - 3) * 3, min((u - 2) * 3, QH)), 1 - par)
                    if ahead and u == 6:
                        qt(T + 1, 0)
                        if not first:
                            pe.wait_ge(v_op, T + 1)
                        qt(T + 1, 1)
                    if ahead and u == 7:
                        qt(T + 1, 2)
                    if not (first and u < 2):
                        pv(T, u - 2, par, 1)

            def after(p, T):
                for u in range(3):
                    ot(T, u - 3, True)
                    if u == 0:
                        pt(T, -1, True)
                    if u < 2:
                        pv(T, u - 2, 0, 1 - u)
                pe.wait_ge(v_otl, T * UN)
                pe.wait_ge(v_op, T)
                op(T - 1, range(0, QH), 1)

            pairs(pe, before, tile, after)

            def l1_tile(t, par, first):
                pe.wait_ge(f_xm, t + 1)
                if not first:
                    pe.wait_ge(f_gelu, t * 2)
                for half in range(2):
                    mm(pS[:, half * HID:(half + 1) * HID], WB[:, par, half, :], XM[:, par, :], start=True, stop=True).then_inc(f_h, 1)
                if not first:
                    pe.wait_ge(f_yb, t)
                for half in range(2):
                    pe.wait_ge(f_gelu, t * 2 + (half + 1))
                    last = mm(pKT[:, :], W2B[:, half, :], HB[:, par, half, :], start=(half == 0), stop=(half == 1))
                last.then_inc(f_y, 1)

            l1_tile(0, 0, True)
            l1_tile(1, 1, False)
            with pe.Fori(1, NT // 2) as i:
                for par in range(2):
                    l1_tile(i * 2 + par, par, False)


def kernel(x, itok_Bx16_0_63, itok_B_207_1644, itok_B_0_7, itok_B_2182_4065, _lenS, L0_cond_Wq, L0_cond_Wk, L0_cond_Wv,
           L0_cond_Wo, L0_cond_q_norm_w, L0_cond_k_norm_w, L0_cond_k_cache, L0_cond_v_cache, L1_cond_W_sess,
           L1_cond_b_sess, L1_cond_W2, L1_cond_b2):
    import concourse.bacc as bacc
    from concourse.bass_utils import run_bass_kernel_spmd

    def c(a):
        return np.ascontiguousarray(a)

    def by_pair(w, n):
        return np.asarray(w).reshape(NP, n, CH, P).transpose(0, 3, 2, 1)

    x2 = np.asarray(x).reshape(NT * P, HID)
    caches = [np.asarray(a).reshape(PAGES, PSIZE, NP, 2 * D).transpose(2, 0, 1, 3) for a in (L0_cond_k_cache, L0_cond_v_cache)]

    def by_batch(a):
        return c(np.asarray(a).reshape(NT, BT).T)

    cst = np.zeros((P, C_ALL), np.float32)
    part, keys = np.arange(P), np.arange(L)
    cst[part, C_ID + part] = 1.0
    cst[:, C_RAMP:C_RAMP + L] = -(keys + 0.5) * BIG
    cst[:, C_FREQ:C_FREQ + HALF] = np.float32(1.0) / np.float32(10000.0) ** (np.arange(0, D, 2, dtype=np.float32) / np.float32(D))
    cst[:, C_IOTA:C_IOTA + L] = keys
    cst[:, C_TOK] = part % S
    cst[:, C_HROW] = part % HID1
    cst[:, C_PAIR:C_PAIR + NP] = np.arange(NP) * (PAGES * PSIZE)

    arrays = {
        "x": c(x2),
        "xT": c(x2.reshape(NT, P, CH, P).transpose(0, 3, 2, 1)),
        "wqkv": c(np.concatenate([by_pair(L0_cond_Wq, QC), by_pair(L0_cond_Wk, KC), by_pair(L0_cond_Wv, VC)], axis=3)),
        "wo": c(np.asarray(L0_cond_Wo).reshape(HID, NP, QH, D).transpose(1, 3, 2, 0)),
        "norm_w": c(np.stack([np.asarray(L0_cond_q_norm_w), np.asarray(L0_cond_k_norm_w)])),
        "kv": c(np.concatenate(caches, axis=3).reshape(NP * PAGES * PSIZE, ROW)),
        "table": c(np.asarray(itok_Bx16_0_63).reshape(B, BLK, BT).transpose(2, 0, 1).reshape(BT, B * BLK)),
        "lens": c(itok_B_207_1644),
        "lens_b": by_batch(itok_B_207_1644),
        "sess_c": by_batch(itok_B_0_7),
        "sess_h": c(np.asarray(itok_B_0_7).reshape(2 * NT, 2).T),
        "chan": by_batch(_lenS),
        "seq": by_batch(itok_B_2182_4065),
        "w_sess": c(np.asarray(L1_cond_W_sess).reshape(N_SESS * MAX_C, HID1)),
        "b_sess": c(np.asarray(L1_cond_b_sess).reshape(N_SESS * HID1, 1)),
        "w2": c(L1_cond_W2),
        "b2": c(np.asarray(L1_cond_b2).reshape(N_SRC, 1)),
        "cst": cst,
    }
    nc = bacc.Bacc("TRN2", target_bir_lowering=False, num_devices=1)
    args = [nc.dram_tensor("in_" + n, a.shape, mybir.dt.from_np(a.dtype), kind="ExternalInput").ap() for n, a in arrays.items()]
    out = nc.dram_tensor("out", (NT, P, HID), F32, kind="ExternalOutput").ap()
    cond_resid_kernel(nc, *args, out)
    r = run_bass_kernel_spmd(nc, [{"in_" + n: a for n, a in arrays.items()}], core_ids=[0])
    return r.results[0]["out"].reshape(B, S, HID)
```

```python
import math
from contextlib import ExitStack

import numpy as np
import concourse.bass as bass
from concourse import mybir

F32, F32R = mybir.dt.float32, mybir.dt.float32r
I32, U32 = mybir.dt.int32, mybir.dt.uint32
ALU = mybir.AluOpType
ACT = mybir.ActivationFunctionType

B, S, HID = 64, 32, 512
D, HQ, HK = 128, 32, 8
PAGES, PSIZE, NPP = 64, 32, 16
L = NPP * PSIZE
KEYS = L + S
P = 128
BT = P // S
NT = B // BT
NP = HK // 2
REP = HQ // HK
QH = 2 * REP
CH = HID // P
BLK = L // P
QC, KC, VC = QH * D, 2 * D, 2 * D
WC = QC + KC + VC
ROW = KC + VC
UN = 2 * BT
PU = UN * NT
SCALE = 1.0 / float(np.sqrt(D))
EPS = 1e-6
BIG = float(2.0 ** 101)
HALF = D // 2
N_SESS, MAX_C, HID1, N_SRC = 8, 32, 64, 32

TURN_PARTS = []
_left = 2 * math.pi
for _ in range(4):
    _unit = 2.0 ** (math.frexp(_left)[1] - 8)
    TURN_PARTS.append(math.floor(_left / _unit) * _unit)
    _left -= TURN_PARTS[-1]
TURN_PARTS.append(_left)
ROUND = 1.5 * 2.0 ** 23
PI_DOWN = 3.1415925

C_ID, C_RAMP, C_FREQ, C_IOTA = 0, P, P + L, P + L + HALF
C_TOK = P + 2 * L + HALF
C_PAIR = C_TOK + 1
C_ALL = C_PAIR + NP


def cond_resid_kernel(nc, x, xT, wqkv, wo, norm_w, kv, table, lens, lens_b, sess_c, sess_b, chan, seq,
                      w_sess, b_sess, w2, b2, cst, out):
    ctx = ExitStack()
    with ctx:
        def sb(name, shape, dt=F32):
            return ctx.enter_context(nc.sbuf_tensor(name, shape, dt))

        def sem(name):
            return ctx.enter_context(nc.semaphore(name))

        WH, WL = sb("WH", [P, CH, WC], F32R), sb("WL", [P, CH, WC], F32R)
        WOH, WOL = sb("WOH", [P, QH, HID], F32R), sb("WOL", [P, QH, HID], F32R)
        XR = sb("XR", [P, CH, P])
        XH, XL = sb("XH", [P, CH, P], F32R), sb("XL", [P, CH, P], F32R)
        KV = sb("KV", [P, BT, BLK, ROW])
        KT = sb("KT", [P, 2, 2, KEYS], F32R)
        PB = sb("PB", [P, 2, KEYS])
        PTS = sb("PTS", [P, 2, BLK, P])
        PN = sb("PN", [P, UN, P])
        OTH, OTL = sb("OTH", [P, 2, QH, P], F32R), sb("OTL", [P, 2, QH, P], F32R)
        QTH = [sb(f"QTH{i}", [P, 2, BT, REP, S], F32R) for i in range(2)]
        QTL = [sb(f"QTL{i}", [P, 2, BT, REP, S], F32R) for i in range(2)]
        KN = sb("KN", [P, 2, 2, 2, P], F32R)
        VN = sb("VN", [P, 2, VC])
        QU = sb("QU", [P, 2 * (QC + KC) + REP * D])
        QN, U, V = QU[:, 0:QC + KC], QU[:, QC + KC:2 * (QC + KC)], QU[:, 2 * (QC + KC):]
        MASK = sb("MASK", [P, 2, KEYS])
        ACC = sb("ACC", [P, HID])
        WOS = sb("WOS", [P, 2 * HID])
        TAB = sb("TAB", [P, 4, D])
        IDENT = sb("IDENT", [P, P])
        RAMP = sb("RAMP", [P, L])
        IDX = sb("IDX", [P, NT * BT * BLK], I32)
        IDXC = sb("IDXC", [P, 2, BT * BLK], U32)
        LENB = sb("LENB", [P, B])
        PAIR = sb("PAIR", [P, NP])
        BIAS, RSUM, RS = sb("BIAS", [P, UN]), sb("RSUM", [P, UN]), sb("RS", [P, UN])
        SS, RV, RSTD = (sb(n, [P, QH + 2]) for n in ("SS", "RV", "RSTD"))
        EXPO = sb("EXPO", [P, REP])
        ANG = PB[:, :, :].rearrange("p i k -> p (i k)")[:, 0:NT * HALF]
        TURNS = PN[:, :, :].rearrange("p u k -> p (u k)")
        SIN = MASK[:, :, :].rearrange("p i k -> p (i k)")[:, 0:NT * HALF]
        TABS = KV[:, :, :, :].rearrange("p b k (c d) -> p (b k) c d", d=D)
        NW = PTS[:, 0, 0:2, :]
        LENP = PTS[:, 1, 0, 0:NT]
        LENI = PTS[:, 1, 1, 0:NT].bitcast(I32)
        LENBI = PTS[:, 1, 2, 0:B].bitcast(I32)
        FREQ = PTS[:, 1, 3, 0:HALF]
        TOK = PTS[:, 1, 3, HALF:HALF + 1]

        KF = KV[:, :, :, :].rearrange("p b k c -> p (b k c)")
        X1 = KF[:, 0:1024].rearrange("p (i n) -> p i n", i=2)
        XM = KF[:, 1024:2048].rearrange("p (i n) -> p i n", i=2)
        HB = KF[:, 2048:4096].rearrange("p (i h n) -> p i h n", i=2, h=2)
        Y = KF[:, 4096:5120].rearrange("p (i n) -> p i n", i=2)
        Z = KF[:, 5120:6144].rearrange("p (i n) -> p i n", i=2)
        WS = QU[:, 0:1024].rearrange("p (t n) -> p t n", t=NT)
        WB = QU[:, 1024:1536].rearrange("p (i h n) -> p i h n", i=2, h=2)
        W2B = QU[:, 1536:1792].rearrange("p (h n) -> p h n", h=2)
        IOTA, BSR = QU[:, 1792:2304], QU[0:B, 2304:2304 + HID1]
        CM, SEQ, BS = QU[:, 2400:2416], QU[:, 2416:2432], QU[:, 2432:2464]
        CHANI, SEQI, SESSC = (QU[:, a:a + NT].bitcast(I32) for a in (2464, 2480, 2496))
        IDXW, SESS = QU[:, 2512:2528].bitcast(U32), QU[0:B, 2528:2529].bitcast(I32)
        ROWS, B2C = QU[:, 2530:2532], QU[:, 2532:2533]
        L1_SESS, L1_PAR = 2 + BT, 1 + 4 * BT
        D_CST = BT + 5

        def bank(name, shape):
            return ctx.enter_context(nc.psum_tensor(name, shape, F32))

        pS = bank("pS", [P, 1024])
        pKT, pPT, pO, pPN = (bank(n, [P, 512]) for n in ("pKT", "pPT", "pO", "pPN"))
        pF = [bank(f"pF{i}", [P, 512]) for i in range(2)]
        SPLIT = KEYS // 2
        pSC = pS[:, :].rearrange("p (i n) -> p i n", i=2)[:, :, 0:SPLIT]

        accd = nc.dram_tensor("accd", (NP + 1, NT, P, HID), F32, kind="Internal").ap()
        tabd = nc.dram_tensor("tabd", (NT, P, 4 * D), F32, kind="Internal").ap()

        d_cst, d_small, d_x0, d_tab, d_xr, d_acc, d_out, d_wo = (
            sem("d_" + n) for n in ("cst", "small", "x0", "tab", "xr", "acc", "out", "wo"))
        d_w = [sem(f"d_w{i}") for i in range(2)]
        d_kv = [sem(f"d_kv{i}") for i in range(BT)]
        d_tabs = [sem(f"d_tabs{i}") for i in range(BT)]
        t_s, t_kt, t_pt, t_pv, t_qkv, t_op, t_qt = (sem("t_" + n) for n in ("s", "kt", "pt", "pv", "qkv", "op", "qt"))
        a_kth, a_pt, a_exp, a_norm, a_oth, a_qkv, a_qth, a_xh, a_wh, a_woh, a_sin = (
            sem("a_" + n) for n in ("kth", "pt", "exp", "norm", "oth", "qkv", "qth", "xh", "wh", "woh", "sin"))
        v_ktl, v_pn, v_max, v_otl, v_rs, v_ss, v_var, v_qn, v_v = (
            sem("v_" + n) for n in ("ktl", "pn", "max", "otl", "rs", "ss", "var", "qn", "v"))
        v_qtl, v_xl, v_wl, v_wol, v_op, v_mask, v_idx, v_angle, v_tabs, v_own = (
            sem("v_" + n) for n in ("qtl", "xl", "wl", "wol", "op", "mask", "idx", "angle", "tabs", "own"))
        g_rstd, g_u, g_rope, g_new = (sem("g_" + n) for n in ("rstd", "u", "rope", "new"))
        v_step, g_step, s_step = (sem(n) for n in ("v_step", "g_step", "s_step"))
        CRED = UN
        e_par, e_sess, e_w, e_b = (sem("e_" + n) for n in ("par", "sess", "w", "b"))
        e_x = [sem(f"e_x{i}") for i in range(2)]
        e_out = [sem(f"e_out{i}") for i in range(2)]
        f_zero, f_idx, f_bt, f_bs, f_xm, f_h, f_gelu, f_y, f_yb, f_m, f_z = (
            sem("f_" + n) for n in ("zero", "idx", "bt", "bs", "xm", "h", "gelu", "y", "yb", "m", "z"))

        block = ctx.enter_context(nc.Block())

        def pairs(e, tile, after):
            def pair(p, T0, nxt):
                tile(p, T0, 0, 0, True, 2, nxt)
                tile(p, T0 + 1, 1, 1, False, 2, nxt)
                with e.Fori(0, (NT - 4) // 2) as i:
                    tile(p, T0 + i * 2 + 2, i * 2 + 2, 0, False, 2, nxt)
                    tile(p, T0 + i * 2 + 3, i * 2 + 3, 1, False, 2, nxt)
                tile(p, T0 + NT - 2, NT - 2, 0, False, 1, nxt)
                tile(p, T0 + NT - 1, NT - 1, 1, False, 0, nxt)
                after(p, T0 + NT, nxt)

            with e.Fori(0, NP - 1) as p:
                pair(p, p * NT, True)
            pair(NP - 1, (NP - 1) * NT, False)

        def done(T, u):
            return T * UN + (u + 1)

        def third(j):
            h0, n = ((QH, 2), (0, REP), (REP, REP))[j]
            return h0, n, slice(h0 * D, (h0 + n) * D)

        PROJ = [[(0, 0, 8)], [(0, 8, 12), (1, 0, 4)], [(1, 4, 12)], [(2, 0, 8)], [(2, 8, 12)], [], [], []]
        PROJ_LAST = [[], [], [], [], [], [(0, 0, 12)], [(1, 0, 12)], [(2, 0, 12)]]
        OUTP = [None] * 4 + [(0, 4), (4, 12), (12, 18), (18, 24)]
        OUTP_LAST = [None, None, (0, 8), (8, 16), (16, 24), None, None, None]

        def slots_of(j, ahead):
            return (1, 2, 4)[j] if ahead else (5, 6, 7)[j]

        def by_head(ap, n):
            return ap.rearrange("p (h d) -> p h d", h=n)

        def o_turned(dst, u, par):
            b, hk = divmod(u, 2)
            return dst[:, par, hk * REP:(hk + 1) * REP, b * S:(b + 1) * S]

        def q_turned(q, part, j, par):
            if j == 0:
                return KN[:, par, part, :, :]
            return q[par][:, j - 1, :, :, :].rearrange("p b h s -> p h b s")

        def f_turned(j):
            if j == 0:
                return pF[0][:, 0:2 * P].rearrange("p (h n) -> p h n", h=2)
            return pF[0][:, :].rearrange("p (h b s) -> p h b s", h=REP, b=BT)

        @block.sync
        def _(sp):
            sp.dma_start(FREQ, cst[:, C_FREQ:C_FREQ + HALF]).then_inc(d_small, 16)
            sp.dma_start(TOK, cst[:, C_TOK:C_TOK + 1], allow_slow_non_contiguous=True).then_inc(d_small, 16)
            for b in range(BT):
                sp.dma_start(LENI[b * S:(b + 1) * S, :], lens_b[b, :].partition_broadcast(S)).then_inc(d_small, 16)

            def load_tab(t):
                sp.dma_start(TAB[:, :, :], tabd[bass.ds(t, 1)].rearrange("a p (c d) -> p (a c) d", d=D)).then_inc(d_tab, 16)

            def load_x(t):
                sp.dma_start(XR[:, :, :], xT[bass.ds(t, 1)].rearrange("a p c n -> p (a c) n")).then_inc(d_xr, 16)

            def load_w(p, c):
                src = wqkv[bass.ds(p, 1), :, c, :].rearrange("a p n -> p (a n)")
                sp.dma_start(QU[:, (c % 2) * WC:(c % 2 + 1) * WC], src).then_inc(d_w[c % 2], 16)

            def load_wo(p, c):
                src = wo[bass.ds(p, 1), :, 2 * c:2 * c + 2, :].rearrange("a p h n -> p (a h n)")
                sp.dma_start(WOS[:, :], src).then_inc(d_wo, 16)

            def acc_in(p, t):
                sp.dma_start(ACC[:, :], accd[bass.ds(p, 1), bass.ds(t, 1)].rearrange("a b p n -> p (a b n)")).then_inc(d_acc, 16)

            def acc_out(p, T, t):
                sp.wait_ge(v_op, T + 2)
                sp.dma_start(accd[bass.ds(p + 1, 1), bass.ds(t, 1)].rearrange("a b p n -> p (a b n)"), ACC[:, :])\
                    .then_inc(d_out, 16)
                sp.wait_ge(d_out, (T + 1) * 16)
                sp.sem_inc(s_step, 1)

            load_w(0, 0)
            load_w(0, 1)
            load_x(0)
            for b in range(BT):
                sp.dma_start(IDX[b * S:(b + 1) * S, :], table[b, :].partition_broadcast(S)).then_inc(d_cst, 16)
            sp.dma_start(PAIR[:, :], cst[:, C_PAIR:C_PAIR + NP]).then_inc(d_cst, 16)
            sp.dma_start(IDENT[:, :], cst[:, C_ID:C_ID + P]).then_inc(d_cst, 16)
            sp.dma_start(RAMP[:, :], cst[:, C_RAMP:C_RAMP + L]).then_inc(d_cst, 16)
            sp.dma_start(NW, norm_w.partition_broadcast(P)).then_inc(d_cst, 16)
            sp.dma_start(LENBI, lens.partition_broadcast(P)).then_inc(d_cst, 16)
            for c in (2, 3):
                sp.wait_ge(v_wl, c - 1)
                load_w(0, c)
            for b in range(BT):
                sp.wait_ge(v_tabs, b + 1)
                sp.dma_start(tabd[b * BT:(b + 1) * BT].rearrange("t p n -> p t n"), KV[:, b, :, :]).then_inc(d_tabs[b], 16)
                if b == 0:
                    sp.wait_ge(v_xl, 1)
                    load_x(1)
                    sp.wait_ge(d_tabs[0], 16)
                    load_tab(0)
            sp.dma_start(accd[0].rearrange("t p n -> (t p) n"), x).then_inc(d_x0, 16)
            sp.wait_ge(d_x0, 16)
            for b in range(1, BT):
                sp.wait_ge(d_tabs[b], 16)

            def tile(p, T, t, par, first, ahead, nxt):
                if ahead:
                    sp.wait_ge(g_rope, T * 3 + 3)
                    load_tab(t + 1)
                if ahead >= 2:
                    sp.wait_ge(v_xl, T + 2)
                    load_x(t + 2)
                if first:
                    for c in range(CH):
                        if c:
                            sp.wait_ge(v_wol, p * CH + c)
                        load_wo(p, c)
                    return
                if ahead == 0 and nxt:
                    sp.wait_ge(v_qtl, T * 3 + 3)
                    load_w(p + 1, 0)
                    load_w(p + 1, 1)
                    load_x(0)
                    load_tab(0)
                if ahead == 0 and not nxt:
                    sp.wait_ge(v_qtl, T * 3 + 3)
                    sp.dma_start(SESS, sess_b, allow_slow_non_contiguous=True).then_inc(e_sess, 16)
                    sp.dma_start(ROWS[:, 0:1], cst[:, C_TOK:C_TOK + 1], allow_slow_non_contiguous=True).then_inc(e_sess, 16)
                    for b in range(BT):
                        sp.dma_start(SESSC[b * S:(b + 1) * S, :], sess_c[b, :].partition_broadcast(S)).then_inc(e_sess, 16)
                if not (isinstance(t, int) and t == 1):
                    acc_out(p, T - 2, t - 2)
                acc_in(p, t - 1)
                if ahead == 0:
                    if nxt:
                        for c in (2, 3):
                            sp.wait_ge(v_wl, (p + 1) * CH + (c - 1))
                            load_w(p + 1, c)
                    acc_out(p, T - 1, t - 1)
                    acc_in(p, t)

            def after(p, T, nxt):
                if nxt:
                    sp.wait_ge(v_xl, T + 1)
                    load_x(1)
                acc_out(p, T - 1, NT - 1)

            pairs(sp, tile, after)

            sp.wait_ge(f_zero, 1)
            sp.dma_start(IOTA, cst[:, C_IOTA:C_IOTA + L]).then_inc(e_par, 16)
            for b in range(BT):
                rows = slice(b * S, (b + 1) * S)
                sp.dma_start(CHANI[rows, :], chan[b, :].partition_broadcast(S)).then_inc(e_par, 16)
                sp.dma_start(SEQI[rows, :], seq[b, :].partition_broadcast(S)).then_inc(e_par, 16)
                sp.dma_start(B2C[rows, :], b2, allow_slow_non_contiguous=True).then_inc(e_par, 16)
                half, odd = divmod(b, 2)
                sp.dma_start(W2B[odd * HID1:(odd + 1) * HID1, half, b * N_SRC:(b + 1) * N_SRC], w2).then_inc(e_par, 16)

            def l1_tile(t, par, first):
                if not first:
                    sp.wait_ge(f_z, t - 1)
                sp.dma_start(X1[:, par, :], accd[NP, bass.ds(t, 1)].rearrange("a p n -> p (a n)")).then_inc(e_x[par], 16)

            def l1_out(t, par):
                sp.wait_ge(f_z, t + 1)
                sp.dma_start(out[bass.ds(t, 1)].rearrange("a p n -> p (a n)"), Z[:, par, :]).then_inc(e_out[par], 16)

            l1_tile(0, 0, True)
            l1_tile(1, 1, True)
            with sp.Fori(0, NT // 2 - 1) as i:
                for par in range(2):
                    l1_out(i * 2 + par, par)
                    l1_tile(i * 2 + (2 + par), par, False)
            for par in range(2):
                l1_out(NT - 2 + par, par)
            for par in range(2):
                sp.wait_ge(e_out[par], NT // 2 * 16)

        @block.gpsimd
        def _(pool):
            def load_kv(T, par, b, blocks):
                if blocks[0] == 0:
                    pool.wait_ge(v_idx, T + 1)
                    pool.wait_ge(t_pv, done(T, 2 * b + 1))
                    pool.sem_inc(g_step, 1)
                for blk in blocks:
                    n = b * BLK + blk
                    nc.gpsimd.indirect_dma_start(
                        out=KV[:, b, blk, :], out_offset=None, in_=kv,
                        in_offset=bass.IndirectOffsetOnAxis(ap=IDXC[:, par, n:n + 1], axis=0)).then_inc(d_kv[b], 16)

            def new_keys(T, u, par, start=False):
                b, hk = divmod(u, 2)
                if u == 0:
                    pool.wait_ge(v_qtl, T * 3 + 1)
                if start and u:
                    pool.wait_ge(v_qtl, T * 3 + 3)
                if not start:
                    pool.wait_ge(t_s, done(T, u - 2))
                pool.sem_inc(g_step, 1)
                nc.gpsimd.tensor_copy(KT[:, u % 2, :, L:KEYS], KN[:, par, :, hk, b * S:(b + 1) * S]).then_inc(g_new, 1)

            def rsqrt(T, j):
                h0, n, _ = third(j)
                pool.wait_ge(v_var, T * 3 + (j + 1))
                nc.gpsimd.tensor_tensor(RSTD[:, h0:h0 + n], RV[:, h0:h0 + n], EXPO[:, 0:n], ALU.pow).then_inc(g_rstd, 1)

            def rope(T, j):
                _, n, cols = third(j)
                u = by_head(U[:, cols], n)
                c = TAB[:, 0 if j else 2, :].unsqueeze(1).to_broadcast([P, n, D])
                pool.wait_ge(d_tab, (T + 1) * 16)
                pool.wait_ge(v_qn, T * 3 + (j + 1))
                nc.gpsimd.tensor_tensor(u, by_head(QN[:, cols], n), c, ALU.mult).then_inc(g_u, 1)
                pool.wait_ge(g_u, T * 3 + (j + 1))
                pool.wait_ge(v_v, T * 3 + (j + 1))
                v = by_head(V[:, 0:n * D], n)
                nc.gpsimd.tensor_tensor(u[:, :, 0:HALF], u[:, :, 0:HALF], v[:, :, HALF:D], ALU.add)
                nc.gpsimd.tensor_tensor(u[:, :, HALF:D], u[:, :, HALF:D], v[:, :, 0:HALF], ALU.add).then_inc(g_rope, 1)

            for b in range(2):
                pool.wait_ge(v_idx, 1)
                pool.wait_ge(d_tabs[b], 16)
                load_kv(0, 0, b, range(BLK))
            for j in range(3):
                rsqrt(0, j)
            for j in range(3):
                rope(0, j)
            new_keys(0, 0, 0, start=True)
            for b in range(2, BT):
                pool.wait_ge(d_tabs[b], 16)

            def tile(p, T, t, par, first, ahead, nxt):
                for u in range(UN):
                    if u < UN - 1:
                        new_keys(T, u + 1, par, start=(first and u == 0))
                    half = range((u % 2) * 2, (u % 2) * 2 + 2)
                    if u < 4:
                        load_kv(T, par, 2 + u // 2, half)
                    elif ahead or nxt:
                        load_kv(T + 1, 1 - par, u // 2 - 2, half)
                    elif u == 4:
                        pool.wait_ge(f_idx, 1)
                        pool.wait_ge(e_sess, L1_SESS * 16)
                        for k in range(NT):
                            nc.gpsimd.indirect_dma_start(
                                out=WS[:, k, :], out_offset=None, in_=w_sess,
                                in_offset=bass.IndirectOffsetOnAxis(ap=IDXW[:, k:k + 1], axis=0)).then_inc(e_w, 16)
                        nc.gpsimd.indirect_dma_start(
                            out=BSR, out_offset=None, in_=b_sess,
                            in_offset=bass.IndirectOffsetOnAxis(ap=SESS.bitcast(U32), axis=0)).then_inc(e_b, 16)
                    if ahead or nxt:
                        for j in range(3):
                            if u == slots_of(j, ahead) + 2:
                                rope(T + 1, j)
                        for j in range(3):
                            if u == slots_of(j, ahead) + 1:
                                rsqrt(T + 1, j)
                        if ahead and u == UN - 1:
                            new_keys(T + 1, 0, 1 - par)

            def after(p, T, nxt):
                if nxt:
                    rope(T, 1)
                    rsqrt(T, 2)
                    rope(T, 2)
                    new_keys(T, 0, 0)

            pairs(pool, tile, after)

        @block.scalar
        def _(act):
            def copy(dst, src, **kw):
                return nc.scalar.activation(dst, src, ACT.Copy, **kw)

            def oth(T, u, par):
                act.wait_ge(t_pv, done(T, u) + CRED)
                copy(o_turned(OTH, u % UN, par if u >= 0 else 1 - par),
                     pO[:, 0:P].rearrange("p (h s) -> p h s", h=REP)).then_inc(a_oth, 1)

            def kth(T, u):
                act.wait_ge(t_kt, done(T, u))
                copy(KT[:, u % 2, 0, 0:L], pKT[:, :]).then_inc(a_kth, 1)

            def pt(T, u):
                act.wait_ge(t_pt, done(T, u))
                copy(PTS[:, u % 2, :, :].rearrange("p k n -> p (k n)"), pPT[:, :]).then_inc(a_pt, 1)

            def exp(T, u):
                act.wait_ge(v_max, done(T, u))
                nc.scalar.activation(PB[:, u % 2, :], PB[:, u % 2, :], ACT.Exp, bias=BIAS[:, u:u + 1], scale=-1.0,
                                     accum_out=RSUM[:, u:u + 1]).then_inc(a_exp, 1)

            def norm(T, u):
                act.wait_ge(v_rs, done(T, u))
                copy(PB[:, u % 2, :], PB[:, u % 2, :], scale=RS[:, u % UN:u % UN + 1]).then_inc(a_norm, 1)

            def projected(T, j, par, start=False):
                act.wait_ge(t_qkv, T * 3 + (j + 1))
                _, n, cols = third(j)
                ev = copy(QN[:, cols], pF[j % 2][:, 0:n * D])
                if j == 0:
                    if not start:
                        act.wait_ge(t_pv, (T - 1) * UN + CRED)
                    ev = copy(VN[:, par, :], pF[0][:, KC:KC + VC])
                ev.then_inc(a_qkv, 1)

            def qth(T, j, par):
                act.wait_ge(t_qt, T * 3 + (j + 1))
                copy(q_turned(QTH, 0, j, par), f_turned(j)).then_inc(a_qth, 1)

            def xh(T, wait_used=True):
                act.wait_ge(d_xr, (T + 1) * 16)
                if wait_used:
                    act.wait_ge(t_qkv, T * 3)
                copy(XH[:, :, :], XR[:, :, :]).then_inc(a_xh, 1)

            def wh(p, c):
                act.wait_ge(d_w[c % 2], (p * 2 + (c // 2 + 1)) * 16)
                copy(WH[:, c, :], QU[:, (c % 2) * WC:(c % 2 + 1) * WC]).then_inc(a_wh, 1)

            def woh(p, c):
                act.wait_ge(d_wo, (p * CH + (c + 1)) * 16)
                copy(WOH[:, 2 * c:2 * c + 2, :].rearrange("p h n -> p (h n)"), WOS[:, :]).then_inc(a_woh, 1)

            xh(0, False)
            wh(0, 0)
            wh(0, 1)
            act.wait_ge(v_angle, 1)
            nc.scalar.activation(SIN, ANG, ACT.Sin).then_inc(a_sin, 1)
            act.wait_ge(v_angle, 2)
            nc.scalar.activation(TURNS, TURNS, ACT.Sin).then_inc(a_sin, 1)
            wh(0, 2)
            wh(0, 3)
            for j in range(3):
                projected(0, j, 0, start=True)
            kth(0, 0)
            qth(0, 0, 0)
            qth(0, 1, 0)
            xh(1)
            qth(0, 2, 0)

            def tile(p, T, t, par, first, ahead, nxt):
                for u in range(UN):
                    if not (first and u < 1):
                        norm(T, u - 1)
                    if not (first and u < 3):
                        oth(T, u - 3, par)
                    if ahead or nxt or u < UN - 1:
                        kth(T, u + 1)
                    if not (first and u < 1):
                        pt(T, u - 1)
                    exp(T, u)
                    if ahead or nxt:
                        for j in range(3):
                            if u == slots_of(j, ahead):
                                projected(T + 1, j, 1 - par)
                    if first and u % 2 == 0:
                        if u == 0:
                            act.wait_ge(t_op, T + 1)
                        woh(p, u // 2)
                    if ahead:
                        if u >= 5:
                            if u == 7 and ahead >= 2:
                                xh(T + 2)
                            qth(T + 1, u - 5, 1 - par)
                    elif nxt and u < 5:
                        if u == 0:
                            xh(T + 1)
                        else:
                            wh(p + 1, u - 1)

            def after(p, T, nxt):
                norm(T, -1)
                oth(T, -3, 0)
                pt(T, -1)
                oth(T, -2, 0)
                if nxt:
                    qth(T, 0, 0)
                oth(T, -1, 0)
                if nxt:
                    xh(T + 1)
                    qth(T, 1, 0)
                    qth(T, 2, 0)

            pairs(act, tile, after)

            act.wait_ge(f_bt, 1)
            for odd in range(2):
                src = pPT[0:HID1, 0:B].rearrange("p (n o) -> p o n", o=2)[:, odd, :]
                copy(BS[odd * HID1:(odd + 1) * HID1, :], src).then_inc(f_bs, 1)
            act.wait_ge(f_bs, 2)
            act.wait_ge(e_par, L1_PAR * 16)

            def l1_gelu(t, par, half):
                act.wait_ge(f_h, t * 2 + (half + 1))
                nc.scalar.activation(HB[:, par, half, :], pS[:, half * HID:(half + 1) * HID], ACT.Gelu,
                                     bias=BS[:, bass.ds(t * 2 + half, 1)]).then_inc(f_gelu, 1)

            def l1_tile(t, par, first):
                for half in range(2):
                    l1_gelu(t, par, half)
                act.wait_ge(f_y, t + 1)
                nc.scalar.activation(Y[:, par, :], pKT[:, :], ACT.Identity, bias=B2C[:, 0:1]).then_inc(f_yb, 1)

            with act.Fori(0, NT // 2) as i:
                for par in range(2):
                    l1_tile(i * 2 + par, par, False)

        @block.vector
        def _(dve):
            chain = [0]

            def link(ins):
                chain[0] += 1
                ins.then_inc(v_own, 1)
                dve.wait_ge(v_own, chain[0])

            def minus(dst, a, hi):
                return nc.vector.tensor_tensor(dst, a, hi.bitcast(F32), ALU.subtract)

            def mask(T, t, b):
                nc.vector.tensor_scalar(MASK[:, b % 2, 0:L], RAMP[:, :], LENB[:, bass.ds(t * BT + b, 1)], 0.0,
                                        ALU.add, ALU.min).then_inc(v_mask, 1)

            def rows(p, t, par):
                nc.vector.tensor_scalar(IDXC[:, par, :], IDX[:, bass.ds(t * (BT * BLK), BT * BLK)],
                                        PAIR[:, bass.ds(p, 1)], None, ALU.add).then_inc(v_idx, 1)

            def masked(T, u):
                dve.wait_ge(t_s, done(T, u))
                dve.wait_ge(v_mask, T * BT + (u // 2 + 1))
                dve.sem_inc(v_step, 1)
                out, m = (a.rearrange("p (i n) -> p i n", i=2) for a in (PB[:, u % 2, :], MASK[:, u // 2 % 2, :]))
                nc.vector.tensor_tensor_reduce(out=out, in0=pSC, in1=m, scale=-SCALE, scalar=3e38, op0=ALU.add, op1=ALU.min,
                                               accum_out=BIAS[:, u:u + 1]).then_inc(v_max, 1)

            def otl(T, u, par):
                dve.wait_ge(a_oth, done(T, u))
                par = par if u >= 0 else 1 - par
                minus(o_turned(OTL, u % UN, par), pO[:, 0:P].rearrange("p (h s) -> p h s", h=REP),
                      o_turned(OTH, u % UN, par)).then_inc(v_otl, 1)

            def ktl(T, u):
                dve.wait_ge(a_kth, done(T, u))
                minus(KT[:, u % 2, 1, 0:L], pKT[:, :], KT[:, u % 2, 0, 0:L]).then_inc(v_ktl, 1)

            def rs(T, u):
                dve.wait_ge(a_exp, done(T, u))
                nc.vector.reciprocal(RS[:, u:u + 1], RSUM[:, u:u + 1]).then_inc(v_rs, 1)

            def pn(T, u):
                dve.wait_ge(t_pt, done(T, u))
                u %= UN
                b = u // 2
                nc.vector.tensor_copy(PN[b * S:(b + 1) * S, u, :], pPN[0:S, 0:P]).then_inc(v_pn, 1)

            def squares(T, j):
                h0, n, _ = third(j)
                dve.wait_ge(a_qkv, T * 3 + (j + 1))
                for h in range(h0, h0 + n):
                    q = QN[:, h * D:(h + 1) * D]
                    last = nc.vector.tensor_tensor_reduce(out=U[:, h * D:(h + 1) * D], in0=q, in1=q, scale=1.0, scalar=0.0,
                                                          op0=ALU.mult, op1=ALU.add, accum_out=SS[:, h:h + 1])
                last.then_inc(v_ss, 1)
                dve.wait_ge(v_ss, T * 3 + (j + 1))
                nc.vector.tensor_scalar(RV[:, h0:h0 + n], SS[:, h0:h0 + n], 1.0 / D, EPS, ALU.mult, ALU.add).then_inc(v_var, 1)

            def normalise(T, j):
                h0, n, cols = third(j)
                dve.wait_ge(g_rstd, T * 3 + (j + 1))
                q = by_head(QN[:, cols], n)
                nc.vector.tensor_tensor(q, q, RSTD[:, h0:h0 + n].unsqueeze(2).to_broadcast([P, n, D]), ALU.mult).then_inc(v_qn, 1)
                dve.wait_ge(v_qn, T * 3 + (j + 1))
                dve.wait_ge(d_tab, (T + 1) * 16)
                if j:
                    dve.wait_ge(g_rope, T * 3 + j)
                s = TAB[:, 1 if j else 3, :].unsqueeze(1).to_broadcast([P, n, D])
                nc.vector.tensor_tensor(by_head(V[:, 0:n * D], n), q, s, ALU.mult).then_inc(v_v, 1)

            def qtl(T, j, par):
                dve.wait_ge(a_qth, T * 3 + (j + 1))
                minus(q_turned(QTL, 1, j, par), f_turned(j), q_turned(QTH, 0, j, par)).then_inc(v_qtl, 1)

            def xl(T):
                dve.wait_ge(a_xh, T + 1)
                minus(XL[:, :, :], XR[:, :, :], XH[:, :, :]).then_inc(v_xl, 1)

            def wl(p, c):
                dve.wait_ge(a_wh, p * CH + (c + 1))
                minus(WL[:, c, :], QU[:, (c % 2) * WC:(c % 2 + 1) * WC], WH[:, c, :]).then_inc(v_wl, 1)

            def wol(p, c):
                dve.wait_ge(a_woh, p * CH + (c + 1))
                heads = slice(2 * c, 2 * c + 2)
                minus(WOL[:, heads, :].rearrange("p h n -> p (h n)"), WOS[:, :],
                      WOH[:, heads, :].rearrange("p h n -> p (h n)")).then_inc(v_wol, 1)

            def add(T):
                dve.wait_ge(d_acc, (T + 1) * 16)
                dve.wait_ge(t_op, T + 2)
                nc.vector.tensor_tensor(ACC[:, :], pF[1][:, :], ACC[:, :], ALU.add).then_inc(v_op, 1)

            link(nc.vector.memset(EXPO[:, :], -0.5))
            dve.sem_inc(v_op, 1)
            dve.wait_ge(d_small, (2 + BT) * 16)
            link(nc.vector.tensor_scalar(LENP, LENI, TOK, None, ALU.add))
            ang3 = ANG.rearrange("p (t f) -> p t f", t=NT)
            link(nc.vector.tensor_tensor(ang3, LENP.unsqueeze(2).to_broadcast([P, NT, HALF]),
                                         FREQ.unsqueeze(1).to_broadcast([P, NT, HALF]), ALU.mult))
            link(nc.vector.tensor_scalar(TURNS, ANG, 1.0 / (2 * math.pi), None, ALU.mult))
            link(nc.vector.tensor_scalar(TURNS, TURNS, ROUND, None, ALU.add))
            link(nc.vector.tensor_scalar(TURNS, TURNS, -ROUND, None, ALU.add))
            for part in TURN_PARTS:
                link(nc.vector.scalar_tensor_tensor(out=ANG, in0=TURNS, scalar=-part, in1=ANG, op0=ALU.mult, op1=ALU.add))
            link(nc.vector.tensor_scalar(ANG, ANG, PI_DOWN, -PI_DOWN, ALU.min, ALU.max))
            dve.sem_inc(v_angle, 1)
            link(nc.vector.scalar_tensor_tensor(out=TURNS, in0=ANG, scalar=-1.0, in1=ANG, op0=ALU.mult, op1=ALU.max))
            link(nc.vector.tensor_scalar(TURNS, TURNS, -1.0, math.pi / 2, ALU.mult, ALU.add))
            dve.sem_inc(v_angle, 1)
            xl(0)
            wl(0, 0)
            wl(0, 1)
            dve.wait_ge(d_cst, D_CST * 16)
            link(nc.vector.tensor_scalar(IDX[:, :], IDX[:, :], float(PSIZE), TOK, ALU.mult, ALU.add))
            link(nc.vector.tensor_scalar(LENB[:, :], LENBI, BIG, None, ALU.mult))
            rows(0, 0, 0)
            dve.wait_ge(a_sin, 2)
            cos3, sin3 = (a.rearrange("p (t f) -> p t f", t=NT) for a in (TURNS, SIN))
            for b in range(BT):
                tiles = slice(b * BT, (b + 1) * BT)
                for w in range(2):
                    for half in range(2):
                        cols = slice(half * HALF, (half + 1) * HALF)
                        wt = NW[:, w, cols].unsqueeze(1).to_broadcast([P, BT, HALF])
                        nc.vector.tensor_tensor(TABS[:, tiles, 2 * w, cols], cos3[:, tiles, :], wt, ALU.mult)
                        last = nc.vector.scalar_tensor_tensor(out=TABS[:, tiles, 2 * w + 1, cols], in0=sin3[:, tiles, :],
                                                              scalar=1.0 - 2.0 * half, in1=wt, op0=ALU.mult, op1=ALU.mult)
                last.then_inc(v_tabs, 1)
                if b == 0:
                    wl(0, 2)
                    wl(0, 3)
            dve.wait_ge(v_tabs, BT)
            link(nc.vector.memset(PN[:, :, :], 0.0))
            link(nc.vector.memset(MASK[:, :, L:KEYS], 0.0))
            mask(0, 0, 0)
            for j in range(3):
                squares(0, j)
            normalise(0, 0)
            normalise(0, 1)
            ktl(0, 0)
            qtl(0, 0, 0)
            normalise(0, 2)
            qtl(0, 1, 0)
            xl(1)
            qtl(0, 2, 0)

            def tile(p, T, t, par, first, ahead, nxt):
                last = ahead == 0
                for u in range(UN):
                    masked(T, u)
                    if not (first and u < 3):
                        otl(T, u - 3, par)
                    if ahead or nxt or u < UN - 1:
                        ktl(T, u + 1)
                    if not (first and u < 1):
                        pn(T, u - 1)
                    if u % 2 and (ahead or u < UN - 1):
                        mask(T, t, u // 2 + 1)
                    if u == 0 and not first and not (isinstance(t, int) and t == 1):
                        add(T - 2)
                    if first and u % 2 == 0:
                        wol(p, u // 2)
                    if ahead:
                        if u == 2:
                            squares(T + 1, 0)
                        if u == 3:
                            squares(T + 1, 1)
                            normalise(T + 1, 0)
                            rows(p, t + 1, 1 - par)
                        if u == 4:
                            normalise(T + 1, 1)
                        if u == 5:
                            squares(T + 1, 2)
                        if u == 6:
                            normalise(T + 1, 2)
                        if u >= 5:
                            qtl(T + 1, u - 5, 1 - par)
                        if u == 7 and ahead >= 2:
                            xl(T + 2)
                    if last and u == 4:
                        add(T - 1)
                    if last and nxt:
                        if u == 0:
                            xl(T + 1)
                        elif u < 5:
                            wl(p + 1, u - 1)
                        if u == 3:
                            rows(p + 1, 0, 0)
                        if u == 6:
                            squares(T + 1, 0)
                        if u == 7:
                            normalise(T + 1, 0)
                            squares(T + 1, 1)
                            mask(T + 1, 0, 0)
                    if last and not nxt:
                        if u == 0:
                            link(nc.vector.memset(W2B[:, :, :], 0.0))
                            link(nc.vector.memset(WB[:, :, :, :], 0.0))
                            dve.sem_inc(f_zero, 1)
                        if u == 3:
                            dve.wait_ge(e_sess, L1_SESS * 16)
                            nc.vector.tensor_scalar(IDXW, SESSC, float(MAX_C), ROWS[:, 0:1], ALU.mult, ALU.add).then_inc(f_idx, 1)
                    rs(T, u)

            def after(p, T, nxt):
                otl(T, -3, 0)
                pn(T, -1)
                if nxt:
                    normalise(T, 1)
                    squares(T, 2)
                otl(T, -2, 0)
                if nxt:
                    qtl(T, 0, 0)
                otl(T, -1, 0)
                if nxt:
                    normalise(T, 2)
                    qtl(T, 1, 0)
                    xl(T + 1)
                add(T - 1)
                if nxt:
                    qtl(T, 2, 0)

            pairs(dve, tile, after)

            dve.wait_ge(e_par, L1_PAR * 16)
            link(nc.vector.tensor_scalar(CM, CHANI, ROWS[:, 0:1], None, ALU.is_gt))
            link(nc.vector.tensor_copy(SEQ, SEQI))
            dve.wait_ge(e_w, NT * 16)

            def l1_in(t, par, first):
                n = slice(0, HID1)
                if not first:
                    dve.wait_ge(f_h, t * 2 - 2)
                for b in range(BT):
                    half, odd = divmod(b, 2)
                    nc.vector.tensor_copy(WB[b * S:(b + 1) * S, par, half, odd * HID1:(odd + 1) * HID1],
                                          WS[b * S:(b + 1) * S, bass.ds(t, 1), n].rearrange("p a n -> p (a n)"))
                dve.wait_ge(e_x[par], (t // 2 + 1) * 16 if isinstance(t, int) else (t - par) * 8 + 16)
                nc.vector.tensor_scalar(XM[:, par, :], X1[:, par, :], CM[:, bass.ds(t, 1)], None, ALU.mult).then_inc(f_xm, 1)

            def l1_out(t, par, first):
                dve.wait_ge(f_yb, t + 1)
                nc.vector.scalar_tensor_tensor(out=Y[:, par, :], in0=IOTA, scalar=SEQ[:, bass.ds(t, 1)], in1=Y[:, par, :],
                                               op0=ALU.is_lt, op1=ALU.mult).then_inc(f_m, 1)
                dve.wait_ge(f_m, t + 1)
                if not first:
                    dve.wait_ge(e_out[par], (t - par) * 8)
                nc.vector.tensor_tensor(Z[:, par, :], Y[:, par, :], X1[:, par, :], ALU.add).then_inc(f_z, 1)

            l1_in(0, 0, True)
            l1_in(1, 1, True)
            for par in range(2):
                l1_out(par, par, True)
                l1_in(2 + par, par, False)
            with dve.Fori(1, NT // 2 - 1) as i:
                for par in range(2):
                    l1_out(i * 2 + par, par, False)
                    l1_in(i * 2 + (2 + par), par, False)
            for par in range(2):
                l1_out(NT - 2 + par, par, False)

        @block.tensor
        def _(pe):
            mm, turn = nc.tensor.matmul, nc.tensor.transpose
            pe.sem_inc(t_pv, CRED)
            pe.sem_inc(t_op, 1)

            def product(dst, terms, steps, total):
                for i in steps:
                    lh, ll, rh, rl = terms[i // 3]
                    a, b = ((lh, rh), (lh, rl), (ll, rh))[i % 3]
                    last = mm(dst, a, b, start=(i == 0), stop=(i == total - 1))
                return last

            def qkv(T, j, lo, hi, wait_bank):
                _, _, cols = third(j)
                if j == 0:
                    cols = slice(cols.start, WC)
                if lo == 0:
                    wait_bank()
                terms = [(XH[:, c, :], XL[:, c, :], WH[:, c, cols], WL[:, c, cols]) for c in range(CH)]
                last = product(pF[j % 2][:, :], terms, range(lo, hi), 3 * CH)
                if hi == 3 * CH:
                    last.then_inc(t_qkv, 1)

            def qkv_free(T, j, first):
                if j == 0:
                    pe.wait_ge(v_xl, T + 2)
                    pe.wait_ge(v_qtl, T * 3 + 3)
                if j == 1:
                    pe.wait_ge(v_op, T + 1 if first else T)
                if j == 2:
                    pe.wait_ge(a_qkv, T * 3 + 4)

            def qt(T, j):
                h0, n, _ = third(j)
                pe.wait_ge(g_rope, T * 3 + (j + 1))
                if j == 0:
                    pe.wait_ge(a_qkv, T * 3 + 3)
                else:
                    pe.wait_ge(v_qtl, T * 3 + j)
                for h in range(n):
                    last = turn(pF[0][:, h * P:(h + 1) * P], U[:, (h0 + h) * D:(h0 + h + 1) * D], IDENT[:, :])
                last.then_inc(t_qt, 1)

            def scores(T, u, par):
                b, hk = divmod(u, 2)
                if u < 2:
                    pe.wait_ge(v_qtl, T * 3 + (u + 2))
                pe.wait_ge(v_ktl, done(T, u))
                pe.wait_ge(g_new, done(T, u))
                qh, ql = (q[par][:, hk, b, :, :].rearrange("p h s -> p (h s)") for q in (QTH, QTL))
                for i in range(2):
                    keys = slice(i * SPLIT, (i + 1) * SPLIT)
                    last = product(pSC[:, i, :], [(qh, ql, KT[:, u % 2, 0, keys], KT[:, u % 2, 1, keys])], range(3), 3)
                last.then_inc(t_s, 1)

            def kt(T, u):
                b, hk = divmod(u % UN, 2)
                if hk == 0:
                    pe.wait_ge(d_kv[b], (T + (1 + u // UN)) * (16 * BLK))
                for k in range(BLK):
                    last = turn(pKT[:, k * P:(k + 1) * P], KV[:, b, k, hk * D:(hk + 1) * D], IDENT[:, :])
                last.then_inc(t_kt, 1)

            def pt(T, u, wait_bank):
                pe.wait_ge(a_norm, done(T, u))
                if wait_bank:
                    pe.wait_ge(a_pt, done(T, u - 1))
                    pe.wait_ge(v_pn, done(T, u - 1))
                for k in range(BLK):
                    turn(pPT[:, k * P:(k + 1) * P], PB[:, u % 2, k * P:(k + 1) * P], IDENT[:, :])
                turn(pPN[0:S, 0:P], PB[:, u % 2, L:KEYS], IDENT[:, :]).then_inc(t_pt, 1)

            def pv(T, u, par, wait_bank=True, wait_p=False):
                if wait_p:
                    pe.wait_ge(a_pt, done(T, u))
                    pe.wait_ge(v_pn, done(T, u))
                if wait_bank:
                    pe.wait_ge(v_otl, done(T, u - 1))
                par = par if u >= 0 else 1 - par
                u %= UN
                b, hk = divmod(u, 2)
                for k in range(BLK):
                    mm(pO[:, 0:P], KV[:, b, k, KC + hk * D:KC + (hk + 1) * D], PTS[:, u % 2, k, :], start=(k == 0), stop=False)
                mm(pO[:, 0:P], VN[:, par, hk * D:(hk + 1) * D], PN[:, u, :], start=False, stop=True).then_inc(t_pv, 1)

            def op(T, par, lo, hi):
                terms = [(OTH[:, par, h, :], OTL[:, par, h, :], WOH[:, h, :], WOL[:, h, :]) for h in range(QH)]
                last = product(pF[1][:, :], terms, range(lo, hi), 3 * QH)
                if hi == 3 * QH:
                    last.then_inc(t_op, 1)

            pe.wait_ge(v_xl, 1)
            pe.wait_ge(v_wl, CH)
            for j in range(3):
                qkv(0, j, 0, 3 * CH, lambda: pe.wait_ge(a_qkv, 1) if j == 2 else None)
            pe.wait_ge(d_cst, D_CST * 16)
            kt(0, 0)
            for j in range(3):
                qt(0, j)

            def tile(p, T, t, par, first, ahead, nxt):
                for u in range(UN):
                    if not (first and u == 0):
                        pe.wait_ge(v_max, done(T, u - 1))
                    scores(T, u, par)
                    if ahead or nxt or u < UN - 1:
                        kt(T, u + 1)
                    if not (first and u < 1):
                        pt(T, u - 1, not (first and u == 1))
                    if ahead or nxt:
                        for j, lo, hi in (PROJ if ahead else PROJ_LAST)[u]:
                            if not ahead and j == 0:
                                pe.wait_ge(v_wl, (p + 1) * CH + CH)
                            qkv(T + 1, j, lo, hi, lambda: qkv_free(T, j, first or not ahead))
                    part = (OUTP if ahead else OUTP_LAST)[u]
                    if part and not first:
                        if part[0] == 0:
                            pe.wait_ge(v_otl, T * UN)
                            if ahead:
                                pe.wait_ge(a_qkv, T * 3 + 5)
                            else:
                                pe.wait_ge(v_op, T)
                            pe.wait_ge(v_wol, p * CH + CH)
                        op(T - 1, 1 - par, *part)
                    if ahead and u >= 5:
                        qt(T + 1, u - 5)
                    if not (first and u < 2):
                        pv(T, u - 2, par, wait_bank=not (first and u == 2))

            def after(p, T, nxt):
                pt(T, -1, True)
                pv(T, -2, 0)
                if nxt:
                    qt(T, 0)
                pv(T, -1, 0, wait_p=True)
                pe.wait_ge(v_otl, T * UN)
                if nxt:
                    pe.wait_ge(a_qkv, T * 3 + 2)
                pe.wait_ge(v_op, T)
                op(T - 1, 1, 0, 12)
                if nxt:
                    qt(T, 1)
                op(T - 1, 1, 12, 3 * QH)
                if nxt:
                    qt(T, 2)

            pairs(pe, tile, after)

            pe.wait_ge(e_b, 16)
            turn(pPT[0:B, 0:HID1], BSR, IDENT[0:B, 0:B]).then_inc(f_bt, 1)

            def l1_tile(t, par, first):
                pe.wait_ge(f_xm, t + 1)
                if not first:
                    pe.wait_ge(f_gelu, t * 2)
                for half in range(2):
                    mm(pS[:, half * HID:(half + 1) * HID], WB[:, par, half, :], XM[:, par, :], start=True, stop=True).then_inc(f_h, 1)
                if not first:
                    pe.wait_ge(f_yb, t)
                for half in range(2):
                    pe.wait_ge(f_gelu, t * 2 + (half + 1))
                    last = mm(pKT[:, :], W2B[:, half, :], HB[:, par, half, :], start=(half == 0), stop=(half == 1))
                last.then_inc(f_y, 1)

            l1_tile(0, 0, True)
            l1_tile(1, 1, False)
            with pe.Fori(1, NT // 2) as i:
                for par in range(2):
                    l1_tile(i * 2 + par, par, False)



def kernel(x, itok_Bx16_0_63, itok_B_207_1644, itok_B_0_7, itok_B_2182_4065, _lenS, L0_cond_Wq, L0_cond_Wk, L0_cond_Wv,
           L0_cond_Wo, L0_cond_q_norm_w, L0_cond_k_norm_w, L0_cond_k_cache, L0_cond_v_cache, L1_cond_W_sess,
           L1_cond_b_sess, L1_cond_W2, L1_cond_b2):
    import concourse.bacc as bacc
    from concourse.bass_utils import run_bass_kernel_spmd

    def c(a):
        return np.ascontiguousarray(a)

    def by_pair(w, n):
        return np.asarray(w).reshape(NP, n, CH, P).transpose(0, 3, 2, 1)

    x2 = np.asarray(x).reshape(NT * P, HID)
    caches = [np.asarray(a).reshape(PAGES, PSIZE, NP, 2 * D).transpose(2, 0, 1, 3) for a in (L0_cond_k_cache, L0_cond_v_cache)]

    def by_batch(a):
        return c(np.asarray(a).reshape(NT, BT).T)

    cst = np.zeros((P, C_ALL), np.float32)
    part, keys = np.arange(P), np.arange(L)
    cst[part, C_ID + part] = 1.0
    cst[:, C_RAMP:C_RAMP + L] = -(keys + 0.5) * BIG
    cst[:, C_FREQ:C_FREQ + HALF] = np.float32(1.0) / np.float32(10000.0) ** (np.arange(0, D, 2, dtype=np.float32) / np.float32(D))
    cst[:, C_IOTA:C_IOTA + L] = keys
    cst[:, C_TOK] = part % S
    cst[:, C_PAIR:C_PAIR + NP] = np.arange(NP) * (PAGES * PSIZE)

    arrays = {
        "x": c(x2),
        "xT": c(x2.reshape(NT, P, CH, P).transpose(0, 3, 2, 1)),
        "wqkv": c(np.concatenate([by_pair(L0_cond_Wq, QC), by_pair(L0_cond_Wk, KC), by_pair(L0_cond_Wv, VC)], axis=3)),
        "wo": c(np.asarray(L0_cond_Wo).reshape(HID, NP, QH, D).transpose(1, 3, 2, 0)),
        "norm_w": c(np.stack([np.asarray(L0_cond_q_norm_w), np.asarray(L0_cond_k_norm_w)])),
        "kv": c(np.concatenate(caches, axis=3).reshape(NP * PAGES * PSIZE, ROW)),
        "table": c(np.asarray(itok_Bx16_0_63).reshape(B, BLK, BT).transpose(2, 0, 1).reshape(BT, B * BLK)),
        "lens": c(itok_B_207_1644),
        "lens_b": by_batch(itok_B_207_1644),
        "sess_c": by_batch(itok_B_0_7),
        "sess_b": c(np.asarray(itok_B_0_7).reshape(B, 1)),
        "chan": by_batch(_lenS),
        "seq": by_batch(itok_B_2182_4065),
        "w_sess": c(np.asarray(L1_cond_W_sess).reshape(N_SESS * MAX_C, HID1)),
        "b_sess": c(L1_cond_b_sess),
        "w2": c(L1_cond_W2),
        "b2": c(np.asarray(L1_cond_b2).reshape(N_SRC, 1)),
        "cst": cst,
    }
    nc = bacc.Bacc("TRN2", target_bir_lowering=False, num_devices=1)
    args = [nc.dram_tensor("in_" + n, a.shape, mybir.dt.from_np(a.dtype), kind="ExternalInput").ap() for n, a in arrays.items()]
    out = nc.dram_tensor("out", (NT, P, HID), F32, kind="ExternalOutput").ap()
    cond_resid_kernel(nc, *args, out)
    r = run_bass_kernel_spmd(nc, [{"in_" + n: a for n, a in arrays.items()}], core_ids=[0])
    return r.results[0]["out"].reshape(B, S, HID)
```

```python
import math
from contextlib import ExitStack

import numpy as np
import concourse.bass as bass
from concourse import mybir

F32, F32R = mybir.dt.float32, mybir.dt.float32r
I32, U32 = mybir.dt.int32, mybir.dt.uint32
ALU = mybir.AluOpType
ACT = mybir.ActivationFunctionType

B, S, HID = 64, 32, 512
D, HQ, HK = 128, 32, 8
PAGES, PSIZE, NPP = 64, 32, 16
L = NPP * PSIZE
KEYS = L + S
P = 128
BT = P // S
NT = B // BT
NP = HK // 2
REP = HQ // HK
QH = 2 * REP
CH = HID // P
BLK = L // P
QC, KC, VC = QH * D, 2 * D, 2 * D
WC = QC + KC + VC
ROW = KC + VC
UN = 2 * BT
SCALE = 1.0 / float(np.sqrt(D))
EPS = 1e-6
BIG = float(2.0 ** 101)
HALF = D // 2
N_SESS, MAX_C, HID1, N_SRC = 8, 32, 64, 32

TURN_PARTS = []
_left = 2 * math.pi
for _ in range(4):
    _unit = 2.0 ** (math.frexp(_left)[1] - 8)
    TURN_PARTS.append(math.floor(_left / _unit) * _unit)
    _left -= TURN_PARTS[-1]
TURN_PARTS.append(_left)
ROUND = 1.5 * 2.0 ** 23
PI_DOWN = 3.1415925

C_ID, C_RAMP, C_FREQ, C_IOTA = 0, P, P + L, P + L + HALF
C_TOK = P + 2 * L + HALF
C_PAIR = C_TOK + 1
C_ALL = C_PAIR + NP


def cond_resid_kernel(nc, x, xT, wqkv, wo, norm_w, kv, table, lens, lens_b, sess_c, sess_b, chan, seq,
                      w_sess, b_sess, w2, b2, cst, out):
    ctx = ExitStack()
    with ctx:
        def sb(name, shape, dt=F32):
            return ctx.enter_context(nc.sbuf_tensor(name, shape, dt))

        def sem(name):
            return ctx.enter_context(nc.semaphore(name))

        WH, WL = sb("WH", [P, CH, WC], F32R), sb("WL", [P, CH, WC], F32R)
        WOH, WOL = sb("WOH", [P, QH, HID], F32R), sb("WOL", [P, QH, HID], F32R)
        XR = sb("XR", [P, CH, P])
        XH, XL = sb("XH", [P, CH, P], F32R), sb("XL", [P, CH, P], F32R)
        KV = sb("KV", [P, BT, BLK, ROW])
        KT = sb("KT", [P, 2, 2, KEYS], F32R)
        PB = sb("PB", [P, 2, KEYS])
        PTS = sb("PTS", [P, 2, BLK, P])
        PN = sb("PN", [P, UN, P])
        OTH, OTL = sb("OTH", [P, 2, QH, P], F32R), sb("OTL", [P, 2, QH, P], F32R)
        QTH = [sb(f"QTH{i}", [P, 2, BT, REP, S], F32R) for i in range(2)]
        QTL = [sb(f"QTL{i}", [P, 2, BT, REP, S], F32R) for i in range(2)]
        KN = sb("KN", [P, 2, 2, 2, P], F32R)
        VN = sb("VN", [P, 2, VC])
        STAGE = sb("STAGE", [P, 2, HID])
        QU = sb("QU", [P, 2 * (QC + KC) + REP * D])
        AREAS = [QU[:, i * 1024:(i + 1) * 1024].rearrange("p (c n) -> p c n", c=2) for i in range(3)] + [STAGE[:, :, :]]
        QN, U, V = QU[:, 0:QC + KC], QU[:, QC + KC:2 * (QC + KC)], QU[:, 2 * (QC + KC):]
        MASK = sb("MASK", [P, 2, KEYS])
        ACC = sb("ACC", [P, HID])
        TAB = sb("TAB", [P, 4, D])
        IDENT = sb("IDENT", [P, P])
        RAMP = sb("RAMP", [P, L])
        IDX = sb("IDX", [P, NT * BT * BLK], I32)
        IDXC = sb("IDXC", [P, 2, BT * BLK], U32)
        LENB = sb("LENB", [P, B])
        PAIR = sb("PAIR", [P, NP])
        BIAS, RSUM, RS = sb("BIAS", [P, UN]), sb("RSUM", [P, UN]), sb("RS", [P, UN])
        SS, RV, RSTD = (sb(n, [P, QH + 2]) for n in ("SS", "RV", "RSTD"))
        EXPO = sb("EXPO", [P, REP])
        TOK = sb("TOK", [P, 1])
        SESSC = sb("SESSC", [P, NT], I32)
        SESS = sb("SESS", [B, 1], I32)
        IDXW = sb("IDXW", [P, NT], U32)
        ANG = PB[:, :, :].rearrange("p i k -> p (i k)")[:, 0:NT * HALF]
        TURNS = PN[:, :, :].rearrange("p u k -> p (u k)")
        SIN = MASK[:, :, :].rearrange("p i k -> p (i k)")[:, 0:NT * HALF]
        TABS = KV[:, 2:4, :, :].rearrange("p b k (c d) -> p b k c d", d=D)
        NW = PTS[:, 0, 0:2, :]
        LENP = PTS[:, 1, 0, 0:NT]
        LENI = PTS[:, 1, 1, 0:NT].bitcast(I32)
        LENBI = PTS[:, 1, 2, 0:B].bitcast(I32)
        FREQ = PTS[:, 1, 3, 0:HALF]

        KF = KV[:, :, :, :].rearrange("p b k c -> p (b k c)")
        X1 = KF[:, 0:2048].rearrange("p (i n) -> p i n", i=4)
        XM = KF[:, 2048:3072].rearrange("p (i n) -> p i n", i=2)
        HB = KF[:, 3072:5120].rearrange("p (i h n) -> p i h n", i=2, h=2)
        Y = KF[:, 5120:6144].rearrange("p (i n) -> p i n", i=2)
        Z = KF[:, 6144:7168].rearrange("p (i n) -> p i n", i=2)
        WS = QU[:, 0:1024].rearrange("p (t n) -> p t n", t=NT)
        WB = QU[:, 1024:1536].rearrange("p (i h n) -> p i h n", i=2, h=2)
        W2B = QU[:, 1536:1792].rearrange("p (h n) -> p h n", h=2)
        IOTA, BSR = QU[:, 1792:2304], QU[0:B, 2304:2304 + HID1]
        CM, SEQ, BS = QU[:, 2400:2416], QU[:, 2416:2432], QU[:, 2432:2464]
        CHANI, SEQI = (QU[:, a:a + NT].bitcast(I32) for a in (2464, 2480))
        B2C = QU[:, 2500:2501]
        L1_SESS, L1_PAR = 1 + BT, 1 + 4 * BT
        D_IDX, D_SMALL, D_CST = BT + 1, BT + 2, 4

        def bank(name, shape):
            return ctx.enter_context(nc.psum_tensor(name, shape, F32))

        pS = bank("pS", [P, 1024])
        pKT, pPT, pO, pPN = (bank(n, [P, 512]) for n in ("pKT", "pPT", "pO", "pPN"))
        pF = [bank(f"pF{i}", [P, 512]) for i in range(2)]
        pH = [[pS[:, 0:HID], pS[:, HID:2 * HID]], [pPT[:, :], pO[:, :]]]
        pY = [pKT, pPN]
        SPLIT = KEYS // 2
        pSC = pS[:, :].rearrange("p (i n) -> p i n", i=2)[:, :, 0:SPLIT]

        accd = nc.dram_tensor("accd", (NP + 1, NT, P, HID), F32, kind="Internal").ap()
        tabd = nc.dram_tensor("tabd", (NT, P, 4 * D), F32, kind="Internal").ap()

        d_idx, d_cst, d_small, d_x0, d_tab, d_xr, d_acc, d_out, d_wo = (
            sem("d_" + n) for n in ("idx", "cst", "small", "x0", "tab", "xr", "acc", "out", "wo"))
        d_w = [sem(f"d_w{i}") for i in range(4)]
        d_kv = [sem(f"d_kv{i}") for i in range(BT)]
        d_tabs = [sem(f"d_tabs{i}") for i in range(BT)]
        t_s, t_kt, t_pt, t_pv, t_qkv, t_op, t_qt = (sem("t_" + n) for n in ("s", "kt", "pt", "pv", "qkv", "op", "qt"))
        a_kth, a_pt, a_exp, a_norm, a_oth, a_qkv, a_qth, a_xh, a_wh, a_woh, a_sin = (
            sem("a_" + n) for n in ("kth", "pt", "exp", "norm", "oth", "qkv", "qth", "xh", "wh", "woh", "sin"))
        v_ktl, v_pn, v_max, v_otl, v_rs, v_ss, v_var, v_qn, v_v = (
            sem("v_" + n) for n in ("ktl", "pn", "max", "otl", "rs", "ss", "var", "qn", "v"))
        v_qtl, v_xl, v_wl, v_wol, v_op, v_mask, v_idx, v_angle, v_tabs, v_own = (
            sem("v_" + n) for n in ("qtl", "xl", "wl", "wol", "op", "mask", "idx", "angle", "tabs", "own"))
        g_rstd, g_u, g_rope, g_new = (sem("g_" + n) for n in ("rstd", "u", "rope", "new"))
        v_step, g_step, s_step = (sem(n) for n in ("v_step", "g_step", "s_step"))
        CRED = UN
        e_par, e_sess, e_w, e_b = (sem("e_" + n) for n in ("par", "sess", "w", "b"))
        e_x = [sem(f"e_x{i}") for i in range(4)]
        e_out = [sem(f"e_out{i}") for i in range(2)]
        f_zero, f_idx, f_bt, f_bs, f_xm, f_h, f_gelu, f_y, f_yb, f_m, f_z = (
            sem("f_" + n) for n in ("zero", "idx", "bt", "bs", "xm", "h", "gelu", "y", "yb", "m", "z"))

        block = ctx.enter_context(nc.Block())

        def pairs(e, tile, after):
            def rest(p, T0, nxt):
                with e.Fori(0, (NT - 4) // 2) as i:
                    tile(p, T0 + i * 2 + 2, i * 2 + 2, 0, 2, nxt)
                    tile(p, T0 + i * 2 + 3, i * 2 + 3, 1, 2, nxt)
                tile(p, T0 + NT - 2, NT - 2, 0, 1, nxt)
                tile(p, T0 + NT - 1, NT - 1, 1, 0, nxt)

            tile(0, 0, 0, 0, 2, True)
            tile(0, 1, 1, 1, 2, True)
            with e.Fori(0, NP - 1) as p:
                rest(p, p * NT, True)
                tile(p + 1, p * NT + NT, 0, 0, 2, True)
                tile(p + 1, p * NT + (NT + 1), 1, 1, 2, True)
            rest(NP - 1, (NP - 1) * NT, False)
            after(NP * NT)

        def known(t):
            return t if isinstance(t, int) else -1

        def done(T, u):
            return T * UN + (u + 1)

        def third(j):
            h0, n = ((QH, 2), (0, REP), (REP, REP))[j]
            return h0, n, slice(h0 * D, (h0 + n) * D)

        PROJ = [[(0, 0, 8)], [(0, 8, 12), (1, 0, 4)], [(1, 4, 12)], [(2, 0, 8)], [(2, 8, 12)], [], [], []]
        PROJ_OPEN = [[], [(0, 0, 12)], [(1, 0, 12)], [(2, 0, 8)], [(2, 8, 12)], [], [], []]
        PROJ_LAST = [[], [], [(0, 0, 8)], [(0, 8, 12), (1, 0, 4)], [(1, 4, 12)], [(2, 0, 12)], [], []]
        OUTP = [None] * 4 + [(0, 4), (4, 12), (12, 18), (18, 24)]
        OUTP_LAST = [None] * 6 + [(0, 12), (12, 24)]
        PIECES = 6
        AREA = (3, 0, 1, 2, 3, 0)
        PIECE_NO = (0, 0, 0, 0, 1, 1)
        PIECES_OF = [[0], [1], [2, 3], [4], [5], [], [], []]
        HEADS = [[0, 1], [], [2, 3], [], [4, 5], [], [6, 7], []]
        SLOTS = {"end": (1, 2, 4), "squares": (2, 3, 5), "normalise": (3, 4, 6), "turn": (5, 6, 7)}
        SLOTS_LAST = {"end": (3, 4, 5), "squares": (4, 5, 6), "normalise": (5, 6, 7), "turn": (6, 7, 8)}

        def thirds(step, u, ahead):
            return [j for j in range(3) if (SLOTS if ahead else SLOTS_LAST)[step][j] == u]

        def piece(w, k):
            j, half = divmod(k, 2)
            cols = slice(QC, WC) if j == 0 else third(j)[2]
            return w[:, 2 * half:2 * half + 2, cols]

        def pieces(p, k):
            return p * PIECES + (k + 1)

        def area_count(p, k):
            if AREA[k] in (0, 3):
                return p * 2 + (PIECE_NO[k] + 1)
            return p + 1

        def by_head(ap, n):
            return ap.rearrange("p (h d) -> p h d", h=n)

        def o_turned(dst, u, par):
            b, hk = divmod(u, 2)
            return dst[:, par, hk * REP:(hk + 1) * REP, b * S:(b + 1) * S]

        def q_turned(q, part, j, par):
            if j == 0:
                return KN[:, par, part, :, :]
            return q[par][:, j - 1, :, :, :].rearrange("p b h s -> p h b s")

        def f_turned(j):
            if j == 0:
                return pF[0][:, 0:2 * P].rearrange("p (h n) -> p h n", h=2)
            return pF[0][:, :].rearrange("p (h b s) -> p h b s", h=REP, b=BT)

        def load_x(e, t):
            e.dma_start(XR[:, :, :], xT[bass.ds(t, 1)].rearrange("a p c n -> p (a c) n")).then_inc(d_xr, 16)

        def load_w(e, p, k):
            src = piece(wqkv[bass.ds(p, 1)].rearrange("a p c n -> p (a c) n"), k)
            e.dma_start(AREAS[AREA[k]], src).then_inc(d_w[AREA[k]], 16)

        @block.sync
        def _(sp):
            sp.dma_start(TOK[:, :], cst[:, C_TOK:C_TOK + 1], allow_slow_non_contiguous=True).then_inc(d_small, 16)
            for b in range(BT):
                sp.dma_start(LENI[b * S:(b + 1) * S, :], lens_b[b, :].partition_broadcast(S)).then_inc(d_small, 16)
            sp.dma_start(FREQ, cst[:, C_FREQ:C_FREQ + HALF]).then_inc(d_small, 16)
            for b in range(BT):
                sp.dma_start(IDX[b * S:(b + 1) * S, :], table[b, :].partition_broadcast(S)).then_inc(d_idx, 16)
            sp.dma_start(PAIR[:, :], cst[:, C_PAIR:C_PAIR + NP]).then_inc(d_idx, 16)
            sp.dma_start(NW, norm_w.partition_broadcast(P)).then_inc(d_cst, 16)
            sp.dma_start(LENBI, lens.partition_broadcast(P)).then_inc(d_cst, 16)
            sp.dma_start(IDENT[:, :], cst[:, C_ID:C_ID + P]).then_inc(d_cst, 16)
            sp.dma_start(RAMP[:, :], cst[:, C_RAMP:C_RAMP + L]).then_inc(d_cst, 16)

            def load_tab(t):
                sp.dma_start(TAB[:, :, :], tabd[bass.ds(t, 1)].rearrange("a p (c d) -> p (a c) d", d=D)).then_inc(d_tab, 16)

            def load_wo(p, c):
                src = wo[bass.ds(p, 1), :, 2 * c:2 * c + 2, :].rearrange("a p h n -> p (a h) n")
                sp.dma_start(STAGE[:, :, :], src).then_inc(d_wo, 16)

            def acc_in(p, t):
                sp.dma_start(ACC[:, :], accd[bass.ds(p, 1), bass.ds(t, 1)].rearrange("a b p n -> p (a b n)")).then_inc(d_acc, 16)

            def acc_out(p, T, t):
                sp.wait_ge(v_op, T + 2)
                sp.dma_start(accd[bass.ds(p + 1, 1), bass.ds(t, 1)].rearrange("a b p n -> p (a b n)"), ACC[:, :])\
                    .then_inc(d_out, 16)
                sp.wait_ge(d_out, (T + 1) * 16)
                sp.sem_inc(s_step, 1)

            def l1_parameters():
                sp.wait_ge(f_zero, 1)
                sp.dma_start(IOTA, cst[:, C_IOTA:C_IOTA + L]).then_inc(e_par, 16)
                for b in range(BT):
                    rows = slice(b * S, (b + 1) * S)
                    sp.dma_start(CHANI[rows, :], chan[b, :].partition_broadcast(S)).then_inc(e_par, 16)
                    sp.dma_start(SEQI[rows, :], seq[b, :].partition_broadcast(S)).then_inc(e_par, 16)
                    sp.dma_start(B2C[rows, :], b2, allow_slow_non_contiguous=True).then_inc(e_par, 16)
                    half, odd = divmod(b, 2)
                    sp.dma_start(W2B[odd * HID1:(odd + 1) * HID1, half, b * N_SRC:(b + 1) * N_SRC], w2).then_inc(e_par, 16)

            def l1_tile(t, k):
                sp.dma_start(X1[:, k, :], accd[NP, bass.ds(t, 1)].rearrange("a p n -> p (a n)")).then_inc(e_x[k], 16)

            for k in (4, 5):
                sp.wait_ge(v_wl, pieces(0, k - 4))
                load_w(sp, 0, k)
            sp.wait_ge(v_xl, 1)
            load_x(sp, 1)
            sp.wait_ge(v_wl, pieces(0, 4))
            load_wo(0, 0)
            for g in range(BT):
                sp.wait_ge(v_tabs, g + 2)
                sp.dma_start(tabd[g * BT:(g + 1) * BT].rearrange("t p n -> p t n"), KV[:, 2 + g % 2, :, :]).then_inc(d_tabs[g], 16)
            sp.dma_start(accd[0].rearrange("t p n -> (t p) n"), x).then_inc(d_x0, 16)
            sp.dma_start(SESS[:, :], sess_b, allow_slow_non_contiguous=True).then_inc(e_sess, 16)
            for b in range(BT):
                sp.dma_start(SESSC[b * S:(b + 1) * S, :], sess_c[b, :].partition_broadcast(S)).then_inc(e_sess, 16)
            for g in range(BT):
                sp.wait_ge(d_tabs[g], 16)

            def tile(p, T, t, par, ahead, nxt):
                if ahead == 0 and nxt:
                    sp.wait_ge(t_qt, T * 3 + 3)
                    sp.sem_inc(s_step, 1)
                if ahead or nxt:
                    sp.wait_ge(g_rope, T * 3 + 3)
                    load_tab(t + 1 if ahead else 0)
                    if ahead == 0:
                        for k in (2, 3):
                            load_w(sp, p + 1, k)
                        sp.wait_ge(v_wl, pieces(p + 1, 0))
                        load_w(sp, p + 1, 4)
                    if ahead >= 2 or nxt:
                        sp.wait_ge(v_xl, T + 2)
                        load_x(sp, t + 2 if ahead >= 2 else 1 - ahead)
                if ahead == 1 and nxt:
                    load_w(sp, p + 1, 0)
                if known(T) == 0:
                    return
                if known(T) == 1:
                    sp.wait_ge(d_x0, 16)
                elif known(t) in (0, 1):
                    acc_out(p - 1, T - 2, t + NT - 2)
                else:
                    acc_out(p, T - 2, t - 2)
                if known(t) == 0:
                    acc_in(p - 1, NT - 1)
                else:
                    acc_in(p, t - 1)
                if known(t) == 1:
                    for c in range(1, CH):
                        sp.wait_ge(v_wol, p * QH + 2 * c)
                        load_wo(p, c)
                if ahead == 1 and nxt:
                    sp.wait_ge(g_rope, T * 3 + 6)
                    sp.sem_inc(s_step, 1)
                    load_w(sp, p + 1, 1)
                if ahead == 0:
                    if nxt:
                        sp.wait_ge(v_wl, pieces(p + 1, 1))
                        load_w(sp, p + 1, 5)
                        sp.wait_ge(v_wl, pieces(p + 1, 4))
                        load_wo(p + 1, 0)
                    else:
                        l1_parameters()
                        sp.wait_ge(t_pv, done(T, 1) + CRED)
                        for k in range(4):
                            l1_tile(k, k)
                        acc_out(p, T - 1, t - 1)
                        acc_in(p, t)

            def after(T):
                acc_out(NP - 1, T - 1, NT - 1)

            pairs(sp, tile, after)

            def l1_out(t, k):
                sp.wait_ge(f_z, t + 1)
                sp.dma_start(out[bass.ds(t, 1)].rearrange("a p n -> p (a n)"), Z[:, k % 2, :]).then_inc(e_out[k % 2], 16)

            with sp.Fori(0, NT // 4 - 1) as i:
                for k in range(4):
                    l1_out(i * 4 + k, k)
                    l1_tile(i * 4 + (4 + k), k)
            for k in range(4):
                l1_out(NT - 4 + k, k)
            for par in range(2):
                sp.wait_ge(e_out[par], NT // 2 * 16)

        @block.gpsimd
        def _(pool):
            def load_kv(T, par, b, blocks):
                if blocks[0] == 0:
                    pool.wait_ge(v_idx, T + 1)
                    pool.wait_ge(t_pv, done(T, 2 * b + 1))
                    if b >= 2:
                        pool.wait_ge(d_tabs[b], 16)
                    pool.sem_inc(g_step, 1)
                for blk in blocks:
                    n = b * BLK + blk
                    nc.gpsimd.indirect_dma_start(
                        out=KV[:, b, blk, :], out_offset=None, in_=kv,
                        in_offset=bass.IndirectOffsetOnAxis(ap=IDXC[:, par, n:n + 1], axis=0)).then_inc(d_kv[b], 16)

            def new_keys(T, u, par, start=False):
                b, hk = divmod(u, 2)
                if u == 0:
                    pool.wait_ge(v_qtl, T * 3 + 1)
                if not start:
                    pool.wait_ge(t_s, done(T, u - 2))
                pool.sem_inc(g_step, 1)
                nc.gpsimd.tensor_copy(KT[:, u % 2, :, L:KEYS], KN[:, par, :, hk, b * S:(b + 1) * S]).then_inc(g_new, 1)

            def rsqrt(T, j):
                h0, n, _ = third(j)
                pool.wait_ge(v_var, T * 3 + (j + 1))
                nc.gpsimd.tensor_tensor(RSTD[:, h0:h0 + n], RV[:, h0:h0 + n], EXPO[:, 0:n], ALU.pow).then_inc(g_rstd, 1)

            def rope(T, j):
                _, n, cols = third(j)
                u = by_head(U[:, cols], n)
                c = TAB[:, 0 if j else 2, :].unsqueeze(1).to_broadcast([P, n, D])
                if isinstance(T, int) and T == 0:
                    pool.wait_ge(v_tabs, 1)
                else:
                    pool.wait_ge(d_tab, T * 16)
                pool.wait_ge(v_qn, T * 3 + (j + 1))
                nc.gpsimd.tensor_tensor(u, by_head(QN[:, cols], n), c, ALU.mult).then_inc(g_u, 1)
                pool.wait_ge(g_u, T * 3 + (j + 1))
                pool.wait_ge(v_v, T * 3 + (j + 1))
                v = by_head(V[:, 0:n * D], n)
                nc.gpsimd.tensor_tensor(u[:, :, 0:HALF], u[:, :, 0:HALF], v[:, :, HALF:D], ALU.add)
                nc.gpsimd.tensor_tensor(u[:, :, HALF:D], u[:, :, HALF:D], v[:, :, 0:HALF], ALU.add).then_inc(g_rope, 1)

            for b in range(2):
                load_kv(0, 0, b, range(BLK))
            rsqrt(0, 0)
            rsqrt(0, 1)
            rope(0, 0)
            rope(0, 1)
            rsqrt(0, 2)
            rope(0, 2)
            new_keys(0, 0, 0, start=True)

            def session_weights(tiles):
                for k in tiles:
                    nc.gpsimd.indirect_dma_start(
                        out=WS[:, k, :], out_offset=None, in_=w_sess,
                        in_offset=bass.IndirectOffsetOnAxis(ap=IDXW[:, k:k + 1], axis=0)).then_inc(e_w, 16)

            def tile(p, T, t, par, ahead, nxt):
                for u in range(UN):
                    if u < UN - 1:
                        new_keys(T, u + 1, par, start=(known(T) == 0 and u == 0))
                    elif ahead or nxt:
                        new_keys(T + 1, 0, 1 - par)
                    half = range((u % 2) * 2, (u % 2) * 2 + 2)
                    if u < 4:
                        load_kv(T, par, 2 + u // 2, half)
                    elif ahead or nxt:
                        load_kv(T + 1, 1 - par, u // 2 - 2, half)
                    if not ahead and not nxt:
                        if u == 0:
                            pool.wait_ge(f_idx, 1)
                            pool.wait_ge(t_qt, T * 3 + 3)
                        session_weights(range(u, u + 1) if u < 4 else range(2 * u - 4, 2 * u - 2))
                    if ahead or nxt:
                        for j in thirds("squares", u, ahead):
                            rsqrt(T + 1, j)
                        for j in thirds("normalise", u, ahead):
                            rope(T + 1, j)

            def after(T):
                session_weights(range(12, NT))
                nc.gpsimd.indirect_dma_start(
                    out=BSR, out_offset=None, in_=b_sess,
                    in_offset=bass.IndirectOffsetOnAxis(ap=SESS[:, :].bitcast(U32), axis=0)).then_inc(e_b, 16)

            pairs(pool, tile, after)

        @block.scalar
        def _(act):
            def copy(dst, src, **kw):
                return nc.scalar.activation(dst, src, ACT.Copy, **kw)

            def oth(T, u, par):
                act.wait_ge(t_pv, done(T, u) + CRED)
                copy(o_turned(OTH, u % UN, par if u >= 0 else 1 - par),
                     pO[:, 0:P].rearrange("p (h s) -> p h s", h=REP)).then_inc(a_oth, 1)

            def kth(T, u):
                act.wait_ge(t_kt, done(T, u))
                copy(KT[:, u % 2, 0, 0:L], pKT[:, :]).then_inc(a_kth, 1)

            def pt(T, u):
                act.wait_ge(t_pt, done(T, u))
                copy(PTS[:, u % 2, :, :].rearrange("p k n -> p (k n)"), pPT[:, :]).then_inc(a_pt, 1)

            def exp(T, u):
                act.wait_ge(v_max, done(T, u))
                nc.scalar.activation(PB[:, u % 2, :], PB[:, u % 2, :], ACT.Exp, bias=BIAS[:, u:u + 1], scale=-1.0,
                                     accum_out=RSUM[:, u:u + 1]).then_inc(a_exp, 1)

            def norm(T, u):
                act.wait_ge(v_rs, done(T, u))
                copy(PB[:, u % 2, :], PB[:, u % 2, :], scale=RS[:, u % UN:u % UN + 1]).then_inc(a_norm, 1)

            def projected(T, j, par, start=False, p=None):
                act.wait_ge(t_qkv, T * 3 + (j + 1))
                if p is not None and j < 2:
                    act.wait_ge(v_wl, pieces(p, (3, 5)[j]))
                _, n, cols = third(j)
                ev = copy(QN[:, cols], pF[j % 2][:, 0:n * D])
                if j == 0:
                    if not start:
                        act.wait_ge(t_pv, (T - 1) * UN + CRED)
                    ev = copy(VN[:, par, :], pF[0][:, KC:KC + VC])
                ev.then_inc(a_qkv, 1)

            def qth(T, j, par):
                act.wait_ge(t_qt, T * 3 + (j + 1))
                copy(q_turned(QTH, 0, j, par), f_turned(j)).then_inc(a_qth, 1)

            def xh(T, wait_used=True):
                act.wait_ge(d_xr, (T + 1) * 16)
                if wait_used:
                    act.wait_ge(t_qkv, T * 3)
                copy(XH[:, :, :], XR[:, :, :]).then_inc(a_xh, 1)

            def wh(p, k):
                act.wait_ge(d_w[AREA[k]], area_count(p, k) * 16)
                copy(piece(WH, k), AREAS[AREA[k]]).then_inc(a_wh, 1)

            def woh(p, h):
                act.wait_ge(d_wo, (p * CH + (h // 2 + 1)) * 16)
                copy(WOH[:, h, :], STAGE[:, h % 2, :]).then_inc(a_woh, 1)

            load_x(act, 0)
            for k in range(4):
                load_w(act, 0, k)
            xh(0, False)
            for k in range(4):
                wh(0, k)
            for k in (4, 5):
                wh(0, k)
            act.wait_ge(v_angle, 1)
            nc.scalar.activation(SIN, ANG, ACT.Sin).then_inc(a_sin, 1)
            act.wait_ge(v_angle, 2)
            nc.scalar.activation(TURNS, TURNS, ACT.Sin).then_inc(a_sin, 1)
            for j in range(3):
                projected(0, j, 0, start=True, p=0)
            kth(0, 0)
            qth(0, 0, 0)
            qth(0, 1, 0)
            xh(1)
            qth(0, 2, 0)

            def tile(p, T, t, par, ahead, nxt):
                first = known(T) == 0
                for u in range(UN):
                    if not (first and u < 3):
                        oth(T, u - 3, par)
                    if ahead or nxt or u < UN - 1:
                        kth(T, u + 1)
                    exp(T, u)
                    if not (first and u < 1):
                        pt(T, u - 1)
                    norm(T, u)
                    if not ahead and nxt:
                        for k in PIECES_OF[u]:
                            wh(p + 1, k)
                    if known(t) == 0 and not first and u == 0:
                        qth(T, 2, par)
                    if known(t) == 1:
                        if u == 0:
                            act.wait_ge(t_op, T)
                        for h in HEADS[u]:
                            woh(p, h)
                    if ahead or nxt:
                        for j in thirds("end", u, ahead):
                            projected(T + 1, j, 1 - par, p=None if ahead else p + 1)
                        for j in thirds("turn", u, ahead):
                            qth(T + 1, j, 1 - par)
                        if u == 7 and (ahead >= 2 or nxt):
                            xh(T + 2)

            def after(T):
                oth(T, -3, 0)
                pt(T, -1)
                oth(T, -2, 0)
                oth(T, -1, 0)

            pairs(act, tile, after)

            act.wait_ge(f_bt, 1)
            for odd in range(2):
                src = pF[0][0:HID1, 0:B].rearrange("p (n o) -> p o n", o=2)[:, odd, :]
                copy(BS[odd * HID1:(odd + 1) * HID1, :], src).then_inc(f_bs, 1)
            act.wait_ge(f_bs, 2)
            act.wait_ge(e_par, L1_PAR * 16)

            def l1_gelu(t, par):
                for half in range(2):
                    act.wait_ge(f_h, t * 2 + (half + 1))
                    nc.scalar.activation(HB[:, par, half, :], pH[par][half], ACT.Gelu,
                                         bias=BS[:, bass.ds(t * 2 + half, 1)]).then_inc(f_gelu, 1)

            def l1_bias(t, par, first=False):
                if not first:
                    act.wait_ge(f_z, t - 1)
                act.wait_ge(f_y, t + 1)
                nc.scalar.activation(Y[:, par, :], pY[par][:, :], ACT.Identity, bias=B2C[:, 0:1]).then_inc(f_yb, 1)

            l1_gelu(0, 0)
            for t in range(4):
                l1_gelu(t + 1, (t + 1) % 2)
                l1_bias(t, t % 2, t < 2)
            with act.Fori(1, NT // 4 - 1) as i:
                for k in range(4):
                    l1_gelu(i * 4 + (k + 1), (k + 1) % 2)
                    l1_bias(i * 4 + k, k % 2)
            for k in range(4):
                if k < 3:
                    l1_gelu(NT - 4 + (k + 1), (k + 1) % 2)
                l1_bias(NT - 4 + k, k % 2)

        @block.vector
        def _(dve):
            chain = [0]

            def link(ins):
                chain[0] += 1
                ins.then_inc(v_own, 1)
                dve.wait_ge(v_own, chain[0])

            def minus(dst, a, hi):
                return nc.vector.tensor_tensor(dst, a, hi.bitcast(F32), ALU.subtract)

            def mask(T, t, b):
                nc.vector.tensor_scalar(MASK[:, b % 2, 0:L], RAMP[:, :], LENB[:, bass.ds(t * BT + b, 1)], 0.0,
                                        ALU.add, ALU.min).then_inc(v_mask, 1)

            def rows(p, t, par):
                nc.vector.tensor_scalar(IDXC[:, par, :], IDX[:, bass.ds(t * (BT * BLK), BT * BLK)],
                                        PAIR[:, bass.ds(p, 1)], None, ALU.add).then_inc(v_idx, 1)

            def masked(T, u):
                dve.wait_ge(t_s, done(T, u))
                dve.wait_ge(v_mask, T * BT + (u // 2 + 1))
                dve.sem_inc(v_step, 1)
                out, m = (a.rearrange("p (i n) -> p i n", i=2) for a in (PB[:, u % 2, :], MASK[:, u // 2 % 2, :]))
                nc.vector.tensor_tensor_reduce(out=out, in0=pSC, in1=m, scale=-SCALE, scalar=3e38, op0=ALU.add, op1=ALU.min,
                                               accum_out=BIAS[:, u:u + 1]).then_inc(v_max, 1)

            def otl(T, u, par):
                dve.wait_ge(a_oth, done(T, u))
                par = par if u >= 0 else 1 - par
                minus(o_turned(OTL, u % UN, par), pO[:, 0:P].rearrange("p (h s) -> p h s", h=REP),
                      o_turned(OTH, u % UN, par)).then_inc(v_otl, 1)

            def ktl(T, u):
                dve.wait_ge(a_kth, done(T, u))
                minus(KT[:, u % 2, 1, 0:L], pKT[:, :], KT[:, u % 2, 0, 0:L]).then_inc(v_ktl, 1)

            def rs(T, u):
                dve.wait_ge(a_exp, done(T, u))
                nc.vector.reciprocal(RS[:, u:u + 1], RSUM[:, u:u + 1]).then_inc(v_rs, 1)

            def pn(T, u):
                dve.wait_ge(t_pt, done(T, u))
                u %= UN
                b = u // 2
                nc.vector.tensor_copy(PN[b * S:(b + 1) * S, u, :], pPN[0:S, 0:P]).then_inc(v_pn, 1)

            def squares(T, j):
                h0, n, _ = third(j)
                dve.wait_ge(a_qkv, T * 3 + (j + 1))
                for h in range(h0, h0 + n):
                    q = QN[:, h * D:(h + 1) * D]
                    last = nc.vector.tensor_tensor_reduce(out=U[:, h * D:(h + 1) * D], in0=q, in1=q, scale=1.0, scalar=0.0,
                                                          op0=ALU.mult, op1=ALU.add, accum_out=SS[:, h:h + 1])
                last.then_inc(v_ss, 1)
                dve.wait_ge(v_ss, T * 3 + (j + 1))
                nc.vector.tensor_scalar(RV[:, h0:h0 + n], SS[:, h0:h0 + n], 1.0 / D, EPS, ALU.mult, ALU.add).then_inc(v_var, 1)

            def normalise(T, j):
                h0, n, cols = third(j)
                dve.wait_ge(g_rstd, T * 3 + (j + 1))
                q = by_head(QN[:, cols], n)
                nc.vector.tensor_tensor(q, q, RSTD[:, h0:h0 + n].unsqueeze(2).to_broadcast([P, n, D]), ALU.mult).then_inc(v_qn, 1)
                dve.wait_ge(v_qn, T * 3 + (j + 1))
                if isinstance(T, int) and T == 0:
                    dve.wait_ge(v_tabs, 1)
                else:
                    dve.wait_ge(d_tab, T * 16)
                if j:
                    dve.wait_ge(g_rope, T * 3 + j)
                s = TAB[:, 1 if j else 3, :].unsqueeze(1).to_broadcast([P, n, D])
                nc.vector.tensor_tensor(by_head(V[:, 0:n * D], n), q, s, ALU.mult).then_inc(v_v, 1)

            def qtl(T, j, par):
                dve.wait_ge(a_qth, T * 3 + (j + 1))
                minus(q_turned(QTL, 1, j, par), f_turned(j), q_turned(QTH, 0, j, par)).then_inc(v_qtl, 1)

            def xl(T):
                dve.wait_ge(a_xh, T + 1)
                minus(XL[:, :, :], XR[:, :, :], XH[:, :, :]).then_inc(v_xl, 1)

            def wl(p, k):
                dve.wait_ge(a_wh, pieces(p, k))
                minus(piece(WL, k), AREAS[AREA[k]], piece(WH, k)).then_inc(v_wl, 1)

            def wol(p, h):
                dve.wait_ge(a_woh, p * QH + (h + 1))
                minus(WOL[:, h, :], STAGE[:, h % 2, :], WOH[:, h, :]).then_inc(v_wol, 1)

            def add(T):
                dve.wait_ge(d_acc, (T + 1) * 16)
                dve.wait_ge(t_op, T + 2)
                nc.vector.tensor_tensor(ACC[:, :], pF[1][:, :], ACC[:, :], ALU.add).then_inc(v_op, 1)

            link(nc.vector.memset(EXPO[:, :], -0.5))
            dve.sem_inc(v_op, 1)
            dve.wait_ge(d_small, D_SMALL * 16)
            link(nc.vector.tensor_scalar(LENP, LENI, TOK[:, 0:1], None, ALU.add))
            ang3 = ANG.rearrange("p (t f) -> p t f", t=NT)
            link(nc.vector.tensor_tensor(ang3, LENP.unsqueeze(2).to_broadcast([P, NT, HALF]),
                                         FREQ.unsqueeze(1).to_broadcast([P, NT, HALF]), ALU.mult))
            link(nc.vector.tensor_scalar(TURNS, ANG, 1.0 / (2 * math.pi), None, ALU.mult))
            link(nc.vector.tensor_scalar(TURNS, TURNS, ROUND, None, ALU.add))
            link(nc.vector.tensor_scalar(TURNS, TURNS, -ROUND, None, ALU.add))
            dve.wait_ge(d_idx, D_IDX * 16)
            link(nc.vector.tensor_scalar(IDX[:, :], IDX[:, :], float(PSIZE), TOK[:, 0:1], ALU.mult, ALU.add))
            rows(0, 0, 0)
            xl(0)
            for k in range(4):
                wl(0, k)
            for part in TURN_PARTS:
                link(nc.vector.scalar_tensor_tensor(out=ANG, in0=TURNS, scalar=-part, in1=ANG, op0=ALU.mult, op1=ALU.add))
            link(nc.vector.tensor_scalar(ANG, ANG, PI_DOWN, -PI_DOWN, ALU.min, ALU.max))
            dve.sem_inc(v_angle, 1)
            link(nc.vector.scalar_tensor_tensor(out=TURNS, in0=ANG, scalar=-1.0, in1=ANG, op0=ALU.mult, op1=ALU.max))
            link(nc.vector.tensor_scalar(TURNS, TURNS, -1.0, math.pi / 2, ALU.mult, ALU.add))
            dve.sem_inc(v_angle, 1)
            for k in range(4, PIECES):
                wl(0, k)
            dve.wait_ge(d_cst, D_CST * 16)
            dve.wait_ge(a_sin, 2)
            cos3, sin3 = (a.rearrange("p (t f) -> p t f", t=NT) for a in (TURNS, SIN))

            def tables(dst, t0, n):
                for w in range(2):
                    for half in range(2):
                        cols = slice(half * HALF, (half + 1) * HALF)
                        wt = NW[:, w, cols].unsqueeze(1).to_broadcast([P, n, HALF])
                        nc.vector.tensor_tensor(dst[:, :, 2 * w, cols], cos3[:, t0:t0 + n, :], wt, ALU.mult)
                        last = nc.vector.scalar_tensor_tensor(out=dst[:, :, 2 * w + 1, cols], in0=sin3[:, t0:t0 + n, :],
                                                              scalar=1.0 - 2.0 * half, in1=wt, op0=ALU.mult, op1=ALU.mult)
                last.then_inc(v_tabs, 1)

            tables(TAB[:, :, :].unsqueeze(1), 0, 1)
            squares(0, 0)
            squares(0, 1)
            normalise(0, 0)
            tables(TABS[:, 0], 0, BT)
            normalise(0, 1)
            squares(0, 2)
            tables(TABS[:, 1], BT, BT)
            qtl(0, 0, 0)
            normalise(0, 2)
            ktl(0, 0)
            qtl(0, 1, 0)
            for g in range(2):
                dve.wait_ge(d_tabs[g], 16)
                tables(TABS[:, g], (2 + g) * BT, BT)
            dve.wait_ge(v_tabs, 1 + BT)
            link(nc.vector.tensor_scalar(LENB[:, :], LENBI, BIG, None, ALU.mult))
            link(nc.vector.memset(PN[:, :, :], 0.0))
            link(nc.vector.memset(MASK[:, :, L:KEYS], 0.0))
            mask(0, 0, 0)
            qtl(0, 2, 0)
            xl(1)

            def tile(p, T, t, par, ahead, nxt):
                first = known(T) == 0
                for u in range(UN):
                    masked(T, u)
                    if not (first and u < 3):
                        otl(T, u - 3, par)
                    if ahead or nxt or u < UN - 1:
                        ktl(T, u + 1)
                    if not (first and u < 1):
                        pn(T, u - 1)
                    if u % 2:
                        if ahead or u < UN - 1:
                            mask(T, t, u // 2 + 1)
                        elif nxt:
                            mask(T + 1, 0, 0)
                    rs(T, u)
                    if known(t) == 0 and not first and u == 0:
                        qtl(T, 2, par)
                    if u == 0 and known(T) not in (0, 1):
                        add(T - 2)
                    if known(t) == 1:
                        for h in HEADS[u]:
                            wol(p, h)
                    if ahead == 0 and nxt:
                        for k in PIECES_OF[u]:
                            wl(p + 1, k)
                    if ahead or nxt:
                        for j in thirds("squares", u, ahead):
                            squares(T + 1, j)
                        for j in thirds("normalise", u, ahead):
                            normalise(T + 1, j)
                        if u == 3:
                            if ahead:
                                rows(p, t + 1, 1 - par)
                            else:
                                rows(p + 1, 0, 0)
                        for j in thirds("turn", u, ahead):
                            qtl(T + 1, j, 1 - par)
                        if u == 7 and (ahead >= 2 or nxt):
                            xl(T + 2)
                    elif u == 0:
                        link(nc.vector.memset(W2B[:, :, :], 0.0))
                        link(nc.vector.memset(WB[:, :, :, :], 0.0))
                        dve.sem_inc(f_zero, 1)
                    elif u == 7:
                        add(T - 1)
                    if not nxt and ahead == 1 and u == 0:
                        dve.wait_ge(e_sess, L1_SESS * 16)
                        nc.vector.tensor_scalar(IDXW[:, :], SESSC[:, :], float(MAX_C), TOK[:, 0:1], ALU.mult, ALU.add)\
                            .then_inc(f_idx, 1)

            def after(T):
                otl(T, -3, 0)
                pn(T, -1)
                otl(T, -2, 0)
                otl(T, -1, 0)
                add(T - 1)

            pairs(dve, tile, after)

            dve.wait_ge(e_par, L1_PAR * 16)
            link(nc.vector.tensor_scalar(CM, CHANI, TOK[:, 0:1], None, ALU.is_gt))
            link(nc.vector.tensor_copy(SEQ, SEQI))
            dve.wait_ge(e_w, NT * 16)

            def l1_in(t, k, group, first):
                par = k % 2
                if not first:
                    dve.wait_ge(f_h, t * 2 - 2)
                for b in range(BT):
                    half, odd = divmod(b, 2)
                    nc.vector.tensor_copy(WB[b * S:(b + 1) * S, par, half, odd * HID1:(odd + 1) * HID1],
                                          WS[b * S:(b + 1) * S, bass.ds(t, 1), 0:HID1].rearrange("p a n -> p (a n)"))
                dve.wait_ge(e_x[k], group * 16 + 16)
                nc.vector.tensor_scalar(XM[:, par, :], X1[:, k, :], CM[:, bass.ds(t, 1)], None, ALU.mult).then_inc(f_xm, 1)

            def l1_out(t, k, first):
                par = k % 2
                dve.wait_ge(f_yb, t + 1)
                nc.vector.scalar_tensor_tensor(out=Y[:, par, :], in0=IOTA, scalar=SEQ[:, bass.ds(t, 1)], in1=Y[:, par, :],
                                               op0=ALU.is_lt, op1=ALU.mult).then_inc(f_m, 1)
                dve.wait_ge(f_m, t + 1)
                if not first:
                    dve.wait_ge(e_out[par], (t - par) * 8)
                nc.vector.tensor_tensor(Z[:, par, :], Y[:, par, :], X1[:, k, :], ALU.add).then_inc(f_z, 1)

            for t in range(2):
                l1_in(t, t, 0, True)
            for t in range(4):
                l1_in(t + 2, (t + 2) % 4, (t + 2) // 4, False)
                l1_out(t, t, t < 2)
            with dve.Fori(1, NT // 4 - 1) as i:
                for k in range(4):
                    l1_in(i * 4 + (k + 2), (k + 2) % 4, i + (k + 2) // 4, False)
                    l1_out(i * 4 + k, k, False)
            for k in range(4):
                if k < 2:
                    l1_in(NT - 4 + (k + 2), k + 2, NT // 4 - 1, False)
                l1_out(NT - 4 + k, k, False)

        @block.tensor
        def _(pe):
            mm, turn = nc.tensor.matmul, nc.tensor.transpose
            pe.sem_inc(t_pv, CRED)
            pe.sem_inc(t_op, 1)

            def product(dst, terms, steps, total):
                for i in steps:
                    lh, ll, rh, rl = terms[i // 3]
                    a, b = ((lh, rh), (lh, rl), (ll, rh))[i % 3]
                    last = mm(dst, a, b, start=(i == 0), stop=(i == total - 1))
                return last

            def qkv(T, j, lo, hi, wait_bank, p=None):
                _, _, cols = third(j)
                if j == 0:
                    cols = slice(cols.start, WC)
                if lo == 0:
                    wait_bank()
                terms = [(XH[:, c, :], XL[:, c, :], WH[:, c, cols], WL[:, c, cols]) for c in range(CH)]
                half = 3 * CH // 2
                for lo, hi in ((lo, min(hi, half)), (max(lo, half), hi)):
                    if lo < hi:
                        if p is not None and lo in (0, half):
                            pe.wait_ge(v_wl, pieces(p, 2 * j + lo // half))
                        last = product(pF[j % 2][:, :], terms, range(lo, hi), 3 * CH)
                if hi == 3 * CH:
                    last.then_inc(t_qkv, 1)

            def qkv_free(T, j):
                if j == 0:
                    pe.wait_ge(v_xl, T + 2)
                    pe.wait_ge(v_qtl, T * 3 + 3)
                if j == 1 and known(T) != 0:
                    pe.wait_ge(v_op, T)
                if j == 2:
                    pe.wait_ge(a_qkv, T * 3 + 4)

            def qt(T, j):
                h0, n, _ = third(j)
                pe.wait_ge(g_rope, T * 3 + (j + 1))
                if j == 0:
                    pe.wait_ge(a_qkv, T * 3 + 3)
                else:
                    pe.wait_ge(v_qtl, T * 3 + j)
                for h in range(n):
                    last = turn(pF[0][:, h * P:(h + 1) * P], U[:, (h0 + h) * D:(h0 + h + 1) * D], IDENT[:, :])
                last.then_inc(t_qt, 1)

            def scores(T, u, par):
                b, hk = divmod(u, 2)
                if u < 2:
                    pe.wait_ge(v_qtl, T * 3 + (u + 2))
                pe.wait_ge(v_ktl, done(T, u))
                pe.wait_ge(g_new, done(T, u))
                qh, ql = (q[par][:, hk, b, :, :].rearrange("p h s -> p (h s)") for q in (QTH, QTL))
                for i in range(2):
                    keys = slice(i * SPLIT, (i + 1) * SPLIT)
                    last = product(pSC[:, i, :], [(qh, ql, KT[:, u % 2, 0, keys], KT[:, u % 2, 1, keys])], range(3), 3)
                last.then_inc(t_s, 1)

            def kt(T, u):
                b, hk = divmod(u % UN, 2)
                if hk == 0:
                    pe.wait_ge(d_kv[b], (T + (1 + u // UN)) * (16 * BLK))
                for k in range(BLK):
                    last = turn(pKT[:, k * P:(k + 1) * P], KV[:, b, k, hk * D:(hk + 1) * D], IDENT[:, :])
                last.then_inc(t_kt, 1)

            def pt(T, u, wait_bank):
                pe.wait_ge(a_norm, done(T, u))
                if wait_bank:
                    pe.wait_ge(a_pt, done(T, u - 1))
                    pe.wait_ge(v_pn, done(T, u - 1))
                for k in range(BLK):
                    turn(pPT[:, k * P:(k + 1) * P], PB[:, u % 2, k * P:(k + 1) * P], IDENT[:, :])
                turn(pPN[0:S, 0:P], PB[:, u % 2, L:KEYS], IDENT[:, :]).then_inc(t_pt, 1)

            def pv(T, u, par, wait_bank=True, wait_p=False):
                if wait_p:
                    pe.wait_ge(a_pt, done(T, u))
                    pe.wait_ge(v_pn, done(T, u))
                if wait_bank:
                    pe.wait_ge(v_otl, done(T, u - 1))
                par = par if u >= 0 else 1 - par
                u %= UN
                b, hk = divmod(u, 2)
                for k in range(BLK):
                    mm(pO[:, 0:P], KV[:, b, k, KC + hk * D:KC + (hk + 1) * D], PTS[:, u % 2, k, :], start=(k == 0), stop=False)
                mm(pO[:, 0:P], VN[:, par, hk * D:(hk + 1) * D], PN[:, u, :], start=False, stop=True).then_inc(t_pv, 1)

            def op(T, par, lo, hi):
                terms = [(OTH[:, par, h, :], OTL[:, par, h, :], WOH[:, h, :], WOL[:, h, :]) for h in range(QH)]
                last = product(pF[1][:, :], terms, range(lo, hi), 3 * QH)
                if hi == 3 * QH:
                    last.then_inc(t_op, 1)

            pe.wait_ge(v_xl, 1)
            for j in range(3):
                qkv(0, j, 0, 3 * CH, lambda: pe.wait_ge(a_qkv, 1) if j == 2 else None, p=0)
            pe.wait_ge(d_cst, D_CST * 16)
            kt(0, 0)
            for j in range(3):
                qt(0, j)

            def tile(p, T, t, par, ahead, nxt):
                first, opening = known(T) == 0, known(t) == 0 and known(T) != 0
                proj = PROJ_OPEN if opening else PROJ if ahead else PROJ_LAST
                outp = OUTP if ahead or not nxt else OUTP_LAST
                for u in range(UN):
                    if not (first and u == 0):
                        pe.wait_ge(v_max, done(T, u - 1))
                    scores(T, u, par)
                    if ahead or nxt or u < UN - 1:
                        kt(T, u + 1)
                    if not (first and u < 1):
                        pt(T, u - 1, not (first and u == 1))
                    if opening and u == 0:
                        qt(T, 2)
                    if ahead or nxt:
                        for j, lo, hi in proj[u]:
                            qkv(T + 1, j, lo, hi, lambda: qkv_free(T, j), p=None if ahead else p + 1)
                    if outp[u] and not first:
                        lo, hi = outp[u]
                        if lo == 0:
                            pe.wait_ge(v_otl, T * UN)
                            if ahead or nxt:
                                pe.wait_ge(a_qkv, T * 3 + 5)
                            else:
                                pe.wait_ge(v_op, T)
                        if known(t) == 1:
                            pe.wait_ge(v_wol, p * QH + -(-hi // 3))
                        op(T - 1, 1 - par, lo, hi)
                    if ahead or nxt:
                        for j in thirds("turn", u, ahead):
                            qt(T + 1, j)
                    if not (first and u < 2):
                        pv(T, u - 2, par, wait_bank=not (first and u == 2))

            def after(T):
                pt(T, -1, True)
                pv(T, -2, 0)
                pv(T, -1, 0, wait_p=True)
                pe.wait_ge(v_otl, T * UN)
                pe.wait_ge(v_op, T)
                op(T - 1, 1, 0, 3 * QH)

            pairs(pe, tile, after)

            pe.wait_ge(e_b, 16)
            turn(pF[0][0:B, 0:HID1], BSR, IDENT[0:B, 0:B]).then_inc(f_bt, 1)

            def l1_hidden(t, par, first):
                pe.wait_ge(f_xm, t + 1)
                if not first:
                    pe.wait_ge(f_gelu, t * 2 - 2)
                for half in range(2):
                    mm(pH[par][half], WB[:, par, half, :], XM[:, par, :], start=True, stop=True).then_inc(f_h, 1)

            def l1_sources(t, par, first):
                if not first:
                    pe.wait_ge(f_yb, t - 1)
                for half in range(2):
                    pe.wait_ge(f_gelu, t * 2 + (half + 1))
                    last = mm(pY[par][:, :], W2B[:, half, :], HB[:, par, half, :], start=(half == 0), stop=(half == 1))
                last.then_inc(f_y, 1)

            l1_hidden(0, 0, True)
            for t in range(4):
                l1_hidden(t + 1, (t + 1) % 2, t == 0)
                l1_sources(t, t % 2, t < 2)
            with pe.Fori(1, NT // 4 - 1) as i:
                for k in range(4):
                    l1_hidden(i * 4 + (k + 1), (k + 1) % 2, False)
                    l1_sources(i * 4 + k, k % 2, False)
            for k in range(4):
                if k < 3:
                    l1_hidden(NT - 4 + (k + 1), (k + 1) % 2, False)
                l1_sources(NT - 4 + k, k % 2, False)


def kernel(x, itok_Bx16_0_63, itok_B_207_1644, itok_B_0_7, itok_B_2182_4065, _lenS, L0_cond_Wq, L0_cond_Wk, L0_cond_Wv,
           L0_cond_Wo, L0_cond_q_norm_w, L0_cond_k_norm_w, L0_cond_k_cache, L0_cond_v_cache, L1_cond_W_sess,
           L1_cond_b_sess, L1_cond_W2, L1_cond_b2):
    import concourse.bacc as bacc
    from concourse.bass_utils import run_bass_kernel_spmd

    def c(a):
        return np.ascontiguousarray(a)

    def by_pair(w, n):
        return np.asarray(w).reshape(NP, n, CH, P).transpose(0, 3, 2, 1)

    x2 = np.asarray(x).reshape(NT * P, HID)
    caches = [np.asarray(a).reshape(PAGES, PSIZE, NP, 2 * D).transpose(2, 0, 1, 3) for a in (L0_cond_k_cache, L0_cond_v_cache)]

    def by_batch(a):
        return c(np.asarray(a).reshape(NT, BT).T)

    cst = np.zeros((P, C_ALL), np.float32)
    part, keys = np.arange(P), np.arange(L)
    cst[part, C_ID + part] = 1.0
    cst[:, C_RAMP:C_RAMP + L] = -(keys + 0.5) * BIG
    cst[:, C_FREQ:C_FREQ + HALF] = np.float32(1.0) / np.float32(10000.0) ** (np.arange(0, D, 2, dtype=np.float32) / np.float32(D))
    cst[:, C_IOTA:C_IOTA + L] = keys
    cst[:, C_TOK] = part % S
    cst[:, C_PAIR:C_PAIR + NP] = np.arange(NP) * (PAGES * PSIZE)

    arrays = {
        "x": c(x2),
        "xT": c(x2.reshape(NT, P, CH, P).transpose(0, 3, 2, 1)),
        "wqkv": c(np.concatenate([by_pair(L0_cond_Wq, QC), by_pair(L0_cond_Wk, KC), by_pair(L0_cond_Wv, VC)], axis=3)),
        "wo": c(np.asarray(L0_cond_Wo).reshape(HID, NP, QH, D).transpose(1, 3, 2, 0)),
        "norm_w": c(np.stack([np.asarray(L0_cond_q_norm_w), np.asarray(L0_cond_k_norm_w)])),
        "kv": c(np.concatenate(caches, axis=3).reshape(NP * PAGES * PSIZE, ROW)),
        "table": c(np.asarray(itok_Bx16_0_63).reshape(B, BLK, BT).transpose(2, 0, 1).reshape(BT, B * BLK)),
        "lens": c(itok_B_207_1644),
        "lens_b": by_batch(itok_B_207_1644),
        "sess_c": by_batch(itok_B_0_7),
        "sess_b": c(np.asarray(itok_B_0_7).reshape(B, 1)),
        "chan": by_batch(_lenS),
        "seq": by_batch(itok_B_2182_4065),
        "w_sess": c(np.asarray(L1_cond_W_sess).reshape(N_SESS * MAX_C, HID1)),
        "b_sess": c(L1_cond_b_sess),
        "w2": c(L1_cond_W2),
        "b2": c(np.asarray(L1_cond_b2).reshape(N_SRC, 1)),
        "cst": cst,
    }
    nc = bacc.Bacc("TRN2", target_bir_lowering=False, num_devices=1)
    args = [nc.dram_tensor("in_" + n, a.shape, mybir.dt.from_np(a.dtype), kind="ExternalInput").ap() for n, a in arrays.items()]
    out = nc.dram_tensor("out", (NT, P, HID), F32, kind="ExternalOutput").ap()
    cond_resid_kernel(nc, *args, out)
    r = run_bass_kernel_spmd(nc, [{"in_" + n: a for n, a in arrays.items()}], core_ids=[0])
    return r.results[0]["out"].reshape(B, S, HID)
```
